# Optimizing a Trainium2 kernel written in Bass

```python
import numpy as np
import jax
import jax.numpy as jnp

def _softmax(x, axis=-1):
    return jax.nn.softmax(x, axis=axis)

def _gelu(x):
    return jax.nn.gelu(x, approximate=True)

def _silu(x):
    return jax.nn.silu(x)

def _sigmoid(x):
    return jax.nn.sigmoid(x)

def _layernorm(x, axis=-1, eps=1e-05):
    m = jnp.mean(x, axis=axis, keepdims=True)
    v = jnp.var(x, axis=axis, keepdims=True)
    return (x - m) / jnp.sqrt(v + eps)

def _scatter_add(tgt, idx, src, axis=0):
    return tgt.at[idx].add(src)

def _segment_sum(src, seg, n):
    return jax.ops.segment_sum(src, seg, n)
kernel_name = 'mk_gnn_resnorm_d2_gnn_r16_3ba587'

def setup_inputs(seed: int=0):
    np.random.seed(seed)
    _w = jnp.asarray

    def _rec_inputs():
        import jax
        import jax.numpy as jnp
        _gk = jax.random.key(seed)
        x = -0.0002117 + 1 * jax.random.normal(jax.random.fold_in(_gk, 1), (625, 512), jnp.float32)
        _s = jax.random.randint(jax.random.fold_in(_gk, 2), (10000,), 0, 625, jnp.int32)
        _d = jax.random.randint(jax.random.fold_in(_gk, 3), (10000,), 0, 625, jnp.int32)
        _loop = jnp.arange(625, dtype=jnp.int32)
        src = jnp.concatenate([_s, _d, _loop])
        dst = jnp.concatenate([_d, _s, _loop])
        _o = jnp.argsort(dst, stable=True)
        src = src[_o]
        dst = dst[_o]
        edge_type_2 = jax.random.randint(jax.random.fold_in(_gk, 12), (20625,), 0, 2, jnp.int32)
        return (x, src, dst, edge_type_2)
    x, src, dst, edge_type_2 = _rec_inputs()

    def _L0_gnn_setup():
        import jax, jax.numpy as jnp
        import numpy as np
        N = 3125
        E = 50000
        D = 512

        def _gcn_conv(x, edge_index, W, b):
            n = x.shape[0]
            xw = x @ W.T
            loop = jnp.arange(n, dtype=edge_index.dtype)
            row = jnp.concatenate([edge_index[0], loop])
            col = jnp.concatenate([edge_index[1], loop])
            deg = jax.ops.segment_sum(jnp.ones_like(row, dtype=xw.dtype), col, num_segments=n)
            dinv = jnp.where(deg > 0, jax.lax.rsqrt(deg), 0.0)
            norm = dinv[row] * dinv[col]
            msgs = norm[:, None] * xw[row]
            out = jax.ops.segment_sum(msgs, col, num_segments=n)
            return out + b

        def _batch_norm(h, gamma, beta, eps=1e-05):
            mean = jnp.mean(h, axis=0)
            var = jnp.var(h, axis=0)
            return (h - mean) * jax.lax.rsqrt(var + eps) * gamma + beta
        key = jax.random.key(seed)
        k1, k2, k3, k4, k5, k6 = jax.random.split(key, 6)
        x = jax.random.normal(k1, (N, D), dtype=jnp.float32)
        edge_index = jax.random.randint(k2, (2, E), 0, N, dtype=jnp.int64)
        W = jax.random.normal(k3, (D, D), dtype=jnp.float32) * (1.0 / np.sqrt(D))
        b = jnp.zeros((D,), dtype=jnp.float32)
        gamma = jnp.ones((D,), dtype=jnp.float32)
        beta = jnp.zeros((D,), dtype=jnp.float32)
        return {'x': x, 'edge_index': edge_index, 'W': W, 'b': b, 'gamma': gamma, 'beta': beta}
    _L0_gnn_all = _L0_gnn_setup()
    _L0_gnn_in = {k: v for k, v in _L0_gnn_all.items() if k in ('W', 'b', 'gamma', 'beta')}
    del _L0_gnn_all

    def _L1_gnn_setup():
        import jax, jax.numpy as jnp
        import numpy as np
        NUM_RELATIONS = 2
        NUM_BASES = 30
        HIDDEN = 512
        N_NODES = 625
        N_EDGES = 10000

        def rgcn_gate_layer(x, row, col, edge_type, basis, att, gate_w, root, bias):
            H = x.shape[1]
            w = jnp.einsum('rb,bio->rio', att, basis)
            x_j = x[col]
            msgs = []
            for r in range(NUM_RELATIONS):
                gate = jax.nn.sigmoid(x_j @ gate_w[r, :, 0])
                msgs.append(gate[:, None] * x_j @ w[r])
            msg = jnp.where((edge_type == 0)[:, None], msgs[0], msgs[1])
            agg = jax.ops.segment_sum(msg, row, num_segments=x.shape[0])
            return agg + x @ root + bias
        key = jax.random.key(seed)
        ks = jax.random.split(key, 16)
        H, R, B = (HIDDEN, NUM_RELATIONS, NUM_BASES)
        bound = 1.0 / np.sqrt(B * H)
        u = lambda k, shape: jax.random.uniform(k, shape, jnp.float32, -bound, bound)
        inp = {'x': jax.random.normal(ks[0], (N_NODES, H), jnp.float32), 'edge_index': jax.random.randint(ks[1], (2, N_EDGES), 0, N_NODES, jnp.int32), 'edge_type': jax.random.randint(ks[2], (N_EDGES,), 0, R, jnp.int32), 'basis1': u(ks[3], (B, H, H)), 'att1': u(ks[4], (R, B)), 'gate_w1': u(ks[5], (R, H, 1)), 'root1': u(ks[6], (H, H)), 'bias1': u(ks[7], (H,)), 'basis2': u(ks[8], (B, H, H)), 'att2': u(ks[9], (R, B)), 'gate_w2': u(ks[10], (R, H, 1)), 'root2': u(ks[11], (H, H)), 'bias2': u(ks[12], (H,))}
        return inp
    _L1_gnn_all = _L1_gnn_setup()
    _L1_gnn_in = {k: v for k, v in _L1_gnn_all.items() if k in ('basis1', 'att1', 'gate_w1', 'root1', 'bias1', 'basis2', 'att2', 'gate_w2', 'root2', 'bias2')}
    del _L1_gnn_all
    return {'x': x, 'src': src, 'dst': dst, 'edge_type_2': edge_type_2, 'L0_gnn_W': _L0_gnn_in['W'], 'L0_gnn_b': _L0_gnn_in['b'], 'L0_gnn_gamma': _L0_gnn_in['gamma'], 'L0_gnn_beta': _L0_gnn_in['beta'], 'L1_gnn_basis1': _L1_gnn_in['basis1'], 'L1_gnn_att1': _L1_gnn_in['att1'], 'L1_gnn_gate_w1': _L1_gnn_in['gate_w1'], 'L1_gnn_root1': _L1_gnn_in['root1'], 'L1_gnn_bias1': _L1_gnn_in['bias1'], 'L1_gnn_basis2': _L1_gnn_in['basis2'], 'L1_gnn_att2': _L1_gnn_in['att2'], 'L1_gnn_gate_w2': _L1_gnn_in['gate_w2'], 'L1_gnn_root2': _L1_gnn_in['root2'], 'L1_gnn_bias2': _L1_gnn_in['bias2']}

def reference(x, src, dst, edge_type_2, L0_gnn_W, L0_gnn_b, L0_gnn_gamma, L0_gnn_beta, L1_gnn_basis1, L1_gnn_att1, L1_gnn_gate_w1, L1_gnn_root1, L1_gnn_bias1, L1_gnn_basis2, L1_gnn_att2, L1_gnn_gate_w2, L1_gnn_root2, L1_gnn_bias2):
    import jax
    import jax.numpy as jnp

    def _L0_gnn_ref(x, edge_index, W, b, gamma, beta):
        import jax, jax.numpy as jnp
        import numpy as np
        N = 3125
        E = 50000
        D = 512

        def _gcn_conv(x, edge_index, W, b):
            n = x.shape[0]
            xw = x @ W.T
            loop = jnp.arange(n, dtype=edge_index.dtype)
            row = jnp.concatenate([edge_index[0], loop])
            col = jnp.concatenate([edge_index[1], loop])
            deg = jax.ops.segment_sum(jnp.ones_like(row, dtype=xw.dtype), col, num_segments=n)
            dinv = jnp.where(deg > 0, jax.lax.rsqrt(deg), 0.0)
            norm = dinv[row] * dinv[col]
            msgs = norm[:, None] * xw[row]
            out = jax.ops.segment_sum(msgs, col, num_segments=n)
            return out + b

        def _batch_norm(h, gamma, beta, eps=1e-05):
            mean = jnp.mean(h, axis=0)
            var = jnp.var(h, axis=0)
            return (h - mean) * jax.lax.rsqrt(var + eps) * gamma + beta
        identity = x
        h = _gcn_conv(x, edge_index, W, b)
        h = _batch_norm(h, gamma, beta)
        h = jax.nn.gelu(h, approximate=False)
        return h + identity

    def _L1_gnn_ref(x, edge_index, edge_type, basis1, att1, gate_w1, root1, bias1, basis2, att2, gate_w2, root2, bias2):
        import jax, jax.numpy as jnp
        import numpy as np
        NUM_RELATIONS = 2
        NUM_BASES = 30
        HIDDEN = 512
        N_NODES = 625
        N_EDGES = 10000

        def rgcn_gate_layer(x, row, col, edge_type, basis, att, gate_w, root, bias):
            H = x.shape[1]
            w = jnp.einsum('rb,bio->rio', att, basis)
            x_j = x[col]
            msgs = []
            for r in range(NUM_RELATIONS):
                gate = jax.nn.sigmoid(x_j @ gate_w[r, :, 0])
                msgs.append(gate[:, None] * x_j @ w[r])
            msg = jnp.where((edge_type == 0)[:, None], msgs[0], msgs[1])
            agg = jax.ops.segment_sum(msg, row, num_segments=x.shape[0])
            return agg + x @ root + bias
        row, col = (edge_index[0], edge_index[1])
        h = jax.nn.relu(rgcn_gate_layer(x, row, col, edge_type, basis1, att1, gate_w1, root1, bias1))
        out = rgcn_gate_layer(h, row, col, edge_type, basis2, att2, gate_w2, root2, bias2)
        return out
    edge_index = jnp.stack([src, dst])
    x = _layernorm(x + _L0_gnn_ref(x, edge_index, L0_gnn_W, L0_gnn_b, L0_gnn_gamma, L0_gnn_beta), axis=-1)
    x = _layernorm(x + _L1_gnn_ref(x, edge_index, edge_type_2, L1_gnn_basis1, L1_gnn_att1, L1_gnn_gate_w1, L1_gnn_root1, L1_gnn_bias1, L1_gnn_basis2, L1_gnn_att2, L1_gnn_gate_w2, L1_gnn_root2, L1_gnn_bias2), axis=-1)
    return x

_drawn_inputs = setup_inputs


def setup_inputs(seed=0):
    import zlib

    import numpy as np

    out = dict(_drawn_inputs(seed))
    spreads = {'L0_gnn_b': (0.0, 0.8), 'L0_gnn_gamma': (1.0, 0.2), 'L0_gnn_beta': (0.0, 0.1)}
    factors = {'L1_gnn_basis1': 8.0,
     'L1_gnn_att1': 8.0,
     'L1_gnn_gate_w1': 8.0,
     'L1_gnn_root1': 8.0,
     'L1_gnn_bias1': 8.0,
     'L1_gnn_basis2': 8.0,
     'L1_gnn_att2': 8.0,
     'L1_gnn_gate_w2': 8.0,
     'L1_gnn_root2': 7.223,
     'L1_gnn_bias2': 8.0}
    for name, (base, spread) in spreads.items():
        noise = np.random.default_rng([zlib.crc32(name.encode()), seed]).standard_normal(out[name].shape)
        drawn = base * np.exp(spread * noise) if base else spread * noise
        out[name] = jnp.asarray(drawn.astype(out[name].dtype))
    for name, factor in factors.items():
        out[name] = (out[name] * factor).astype(out[name].dtype)
    return out
```

```python
from contextlib import ExitStack

import numpy as np

import concourse.bass as bass
from concourse import mybir

F32 = mybir.dt.float32
F32R = mybir.dt.float32r
F16 = mybir.dt.float16
BF16 = mybir.dt.bfloat16
U16 = mybir.dt.uint16
I32 = mybir.dt.int32
ALU = mybir.AluOpType
ACT = mybir.ActivationFunctionType
AX = mybir.AxisListType

P = 128
N = 625
D = 512
E = 20625
NB = 30
R = 2
PC = 125
NC = N // PC
KC = D // P
N2 = N + 1
HALF = ((0, 320), (320, N2 - 320))
T = -(-E // P)
G = 8
NG = -(-T // G)
W = 48
WIN = R * W
BW = N - 1 + W
FULL = (E // P) * P
KB = 4
PB = NB * KB
CH = 8
SUB = 4
RING = 4
OH = 6
WBLK = 6
EPS = 1e-5


def gnn_block(nc, x, src, dst, etype, W0, b0, gamma, beta,
              basis1, att1, gate1, root1, bias1, basis2, att2, gate2, root2, bias2, out):
    ctx = ExitStack()

    def sem(name):
        return ctx.enter_context(nc.semaphore(name))

    def sb(name, shape, dt, scope=ctx):
        return scope.enter_context(nc.sbuf_tensor(name, shape, dt))

    def share(*phases):
        def length(tensors):
            return sum(int(np.prod(shape[1:])) * (2 if dt in (F16, BF16, U16) else 4) for _, shape, dt in tensors)

        made = {}
        for i, tensors in enumerate(phases):
            scope = ctx if i == len(phases) - 1 else ExitStack()
            for name, shape, dt in tensors:
                made[name] = sb(name, shape, dt, scope)
            if scope is ctx:
                rest = max(map(length, phases)) - length(tensors)
                if rest:
                    sb(f"after_{name}", [P, -(-rest // 4)], F32)
            else:
                scope.close()
        return made

    with ctx:
        reg_r = share([("basis_ring", [P, RING, SUB, D], F32)], [("res", [PC, NC, D], F32)])
        ring, res = reg_r["basis_ring"], reg_r["res"]
        stage = sb("w_stage", [P, 2, 2, D], F32R)
        w_old = share([("oh_src", [P, OH, 640], F16), ("oh_diff", [P, 2, G * WIN], F16),
                       ("oh_win", [P, 2, G * WIN], F16)],
                      [("w45", [P, 2, R, 2, D], F32R)])
        oh_src, oh_diff, oh_win, w45 = (w_old[n] for n in ("oh_src", "oh_diff", "oh_win", "w45"))
        w03 = sb("w03", [P, 4, R, 2, D], F32R)
        reg_b = share([("w0_raw", [P, KC, D], F32), ("xw", [PC, NC, D], F32), ("rows_i", [P, 3, P], I32)],
                      [("BB", [PC, NC * R * N + 6], F32R)])
        w0_raw, xw, rows_i, BB = (reg_b[n] for n in ("w0_raw", "xw", "rows_i", "BB"))
        reg_x = share([("B", [PC, NC, R, BW], U16), ("edgeT", [P, 3, T], F32), ("key", [P, T], F32),
                       ("key2", [P, T], F32), ("base_b", [P, NG], F32), ("tail_f", [T - P, 3, P], F32),
                       ("beyond", [P, T], F32)],
                      [("hlT", [P, 2, KC, N2], F32R)])
        B, edgeT, key, key2, base_b, tail_f, beyond, hlT = (
            reg_x[n] for n in ("B", "edgeT", "key", "key2", "base_b", "tail_f", "beyond", "hlT"))
        reg_z = share([("xT_full", [P, KC, N2], F32)],
                      [("xT_lo", [P, KC, N2], F32R), ("xT_hi", [P, KC, N2], F32R)],
                      [("z", [PC, 2, NC, D], F32R), ("AT", [PC, NC, N2], F32R),
                       ("dinv_b", [P, N2], F32), ("diag", [PC, NC, PC], F32)],
                      [("root1_raw", [P, KC, D], F32), ("x_sum", [PC, NC, D], F32),
                       ("root1_lo", [P, KC, D], F32R), ("root1_hi", [P, KC, D], F32R)],
                      [("zg", [PC, 2, NC, R, D], F32R)])
        xT_full, xT_lo, xT_hi, z, AT, dinv_b, diag, root1_raw, x_sum, root1_lo, root1_hi, zg = (
            reg_z[n] for n in ("xT_full", "xT_lo", "xT_hi", "z", "AT", "dinv_b", "diag", "root1_raw", "x_sum", "root1_lo", "root1_hi", "zg"))
        reg_q = share([("w0T_full", [P, KC, D], F32)],
                      [("w0T_lo", [P, KC, D], F32R), ("w0T_hi", [P, KC, D], F32R)], [("hf", [P, KC, N], F32)],
                      [("r1T", [P, KC, N], F32)], [("root2_raw", [P, KC, D], F32)],
                      [("root2_lo", [P, KC, D], F32R), ("root2_hi", [P, KC, D], F32R)])
        w0T_full, w0T_lo, w0T_hi, hf, r1T, root2_raw, root2_lo, root2_hi = (
            reg_q[n] for n in ("w0T_full", "w0T_lo", "w0T_hi", "hf", "r1T", "root2_raw", "root2_lo", "root2_hi"))
        xs = sb("xs", [PC, NC, D], F32)
        reg_e = share([("rows_f", [P, 3, P], F32), ("tail_i", [T - P, 3, P], I32)],
                      [("tile_f", [1, T], F32), ("tile_i", [1, T], I32)], [("bias2_b", [PC, D], F32)])
        rows_f, tail_i, tile_f, tile_i, bias2_b = (reg_e[n] for n in ("rows_f", "tail_i", "tile_f", "tile_i", "bias2_b"))

        ident = sb("ident", [P, P], F32)
        ident16 = sb("ident16", [P, P], BF16)
        iota_f = sb("iota_f", [P, 640], F16)
        ones_r = sb("ones_r", [PC, P], F32R)
        ones_f = sb("ones_f", [P, P], F32)
        mm = sb("mm", [P, 2, 2], F32)
        gmm = sb("gmm", [1, 4, NG], F32)
        base_i = sb("base_i", [1, NG], I32)
        spans = sb("spans", [1, 16], F32)
        more_f = sb("more_f", [1, 1], F32)
        more_i = sb("more_i", [1, 1], I32)
        attp = sb("attp", [PB, 2, R], F32)
        mask4 = sb("mask4", [PB, KB], F32)
        S = sb("S", [PB, 2, SUB, 32], F32)
        gw = sb("gw", [P, 2, KC, R], F32)
        gw_hl = sb("gw_hl", [P, 2, 2, KC, R], F32R)
        vec0 = sb("vec0", [P, 3, KC], F32)
        bias1_q = sb("bias1_q", [P, KC], F32)
        deg = sb("deg", [PC, NC], F32)
        mhalf = sb("mhalf", [P, NC], F32)
        dinv_p = sb("dinv_p", [PC, NC], F32)
        bst = sb("bst", [P, KC, 2, 6], F32)
        bag = sb("bag", [P, KC, 2], F32)
        bn = sb("bn", [P, 4, KC], F32)
        lst = sb("lst", [PC, NC, 6], F32)
        lag = sb("lag", [PC, NC, 2], F32)
        lrs = sb("lrs", [PC, NC], F32)
        gate = sb("gate", [PC, 2, NC, R], F32)

        psM = ctx.enter_context(nc.psum_tensor("psM", [P, 4, 512], F32))
        psE = ctx.enter_context(nc.psum_tensor("psE", [P, 2, 512], F32))
        psW = ctx.enter_context(nc.psum_tensor("psW", [P, 2, 512], F32))

        rows_set = sem("rows_set")
        edges_in = sem("edges_in")
        x_in, w0_in, small_in = sem("x_in"), sem("w0_in"), sem("small_in")
        root1_in, root2_in, bias2_in = sem("root1_in"), sem("root2_in"), sem("bias2_in")
        basis_in = [sem(f"basis_in{i}") for i in range(RING)]
        basis_used = sem("basis_used")
        w_hi, w_lo = sem("w_hi"), sem("w_lo")
        w_moved = [sem(f"w_moved{i}") for i in range(2)]
        consts = sem("consts")
        round_step, gen_ready, gen_used, gen_added = (
            sem("round_step"), sem("gen_ready"), sem("gen_used"), sem("gen_added"))
        pchain = sem("pchain")
        ident_in = sem("ident_in")
        main_full = sem("main_full")
        free_act, free_dve = sem("free_act"), sem("free_dve")
        vchain = sem("vchain")
        achain = sem("achain")
        rows_ready = sem("rows_ready")
        minmax_ready = sem("minmax_ready")
        base_ready = sem("base_ready")
        key_ready = sem("key_ready")
        diff_ready, win_ready = sem("diff_ready"), sem("win_ready")
        src_ready, adj_used = sem("src_ready"), sem("adj_used")
        win_added = sem("win_added")
        in_lo, in_hi = sem("in_lo"), sem("in_hi")
        xw_ready = sem("xw_ready")
        at_ready, dinv_ready = sem("at_ready"), sem("dinv_ready")
        z_hi, z_ready = sem("z_hi"), sem("z_ready")
        deg_ready, diag_ready = sem("deg_ready"), sem("diag_ready")
        var_ready, rstd_ready = sem("var_ready"), sem("rstd_ready")
        bn_ready, gelu_done = sem("bn_ready"), sem("gelu_done")
        bb_ready = sem("bb_ready")
        x1_ready = sem("x1_ready")
        t_hi, t_ready = sem("t_hi"), sem("t_ready")
        root_hi, root_ready = sem("root_hi"), sem("root_ready")
        r1_ready = sem("r1_ready")
        gate_ready = sem("gate_ready")
        zg_hi, zg_ready = sem("zg_hi"), sem("zg_ready")
        h_sum = sem("h_sum")
        o_ready, out_done = sem("o_ready"), sem("out_done")
        x_pe = {}

        uses, releaser = {}, []

        def use(name, by):
            uses[name] = len(releaser)
            releaser.append(by)

        for a in range(3):
            use(("edge", a), "dve")
        use("minmax", "dve")
        for c in range(NC):
            use(("xT", c), "act")
        use("base", "dve")
        for k in range(KC):
            use(("w0T", k), "act")
        for c in range(NC):
            use(("xw", c), "act")
        use("deg", "dve")
        for h in range(2):
            use(("dinv", h), "dve")
        for f in range(KC):
            for h in range(2):
                use(("agg0", f, h), "dve")
        NBB = -(-NC * R * NC // 4)
        for b in range(NBB):
            use(("bb", b), "act")
        for c in range(NC):
            use(("g", c), "dve")
        for c in range(NC):
            use(("x1T", c), "dve")
        for f in range(KC):
            for h in range(2):
                use(("root1", f, h), "act")
        for L in range(2):
            use(("gate", L), "act")
            for c in range(NC):
                for r in range(R):
                    use(("Z", L, c, r), "dve")
            if L == 0:
                for f in range(KC):
                    for h in range(2):
                        use(("h", f, h), "dve")
        for c in range(NC):
            use(("out", c), "dve")

        def bank(name):
            return psM[:, uses[name] % 4, :]

        def wait_full(eng, name):
            eng.wait_ge(main_full, uses[name] + 1)

        def release(ins, name, by):
            assert releaser[uses[name]] == by
            ins.then_inc(free_act if by == "act" else free_dve, 1)

        def wait_free(pe, name):
            before = uses[name] - 4
            if before >= 0:
                by = releaser[before]
                pe.wait_ge(free_act if by == "act" else free_dve, releaser[:before + 1].count(by))

        def natural(ap):
            return ap.rearrange("p (k c u) -> p c u k", k=KB, c=KC)

        def in_q(ap):
            return ap.rearrange("p (c u k) -> p c u k", k=KB, c=KC)

        def q_as_natural(ap):
            return ap.rearrange("p (c u k) -> p k c u", k=KB, c=KC)

        def w_block(L, kc):
            b = L * KC + kc
            return w03[:, b % WBLK] if b % WBLK < 4 else w45[:, b % WBLK - 4]

        block = ctx.enter_context(nc.Block())

        @block.sync
        def _(sp):
            def load(n):
                L, c, g = n // (CH * SUB), n // SUB % CH, n % SUB
                if n >= RING:
                    sp.wait_ge(basis_used, n - RING + 1)
                rows = (basis1, basis2)[L].rearrange("b (k c j g) o -> (b k) c g j o", k=KB, c=CH, j=4, g=SUB)
                sp.dma_start(ring[0:PB, n % RING], rows[:, c, g]).then_inc(basis_in[n % RING], 16)

            def move(cc):
                L, c = cc // CH, cc % CH
                sp.wait_ge(w_lo, cc + 1)
                if L * KC + c // 2 >= WBLK:
                    sp.wait_ge(main_full, uses[("Z", 0, NC - 1, R - 1)] + 1)
                elif L * KC + c // 2 >= 4:
                    sp.wait_ge(adj_used, T)
                for r in range(R):
                    for j in range(4):
                        sp.dma_start(w_block(L, c // 2)[64 * (c % 2) + 16 * j:64 * (c % 2) + 16 * j + 16, r]
                                     .bitcast(F32),
                                     stage[32 * j + 16 * r:32 * j + 16 * r + 16, cc % 2].bitcast(F32)
                                     ).then_inc(w_moved[cc % 2], 16)

            for n in range(2 * CH * SUB):
                load(n)
                if n >= SUB and n % SUB == SUB - 1:
                    move(n // SUB - 1)
            move(2 * CH - 1)
            for c in range(NC):
                sp.wait_ge(o_ready, c + 1)
                sp.dma_start(out.rearrange("(c p) o -> p c o", p=PC)[:, c], xs[:, c]).then_inc(out_done, 16)
            sp.wait_ge(out_done, 16 * NC)

        @block.gpsimd
        def _(pool):
            chained = [0]

            def link(ins):
                chained[0] += 1
                ins.then_inc(pchain, 1)
                pool.wait_ge(pchain, chained[0])

            nt = T - P
            nc.gpsimd.memset(tail_i[:, 0, :], -1).then_inc(rows_set, 1)
            nc.gpsimd.memset(tail_i[:, 1, :], N - 1).then_inc(rows_set, 1)
            nc.gpsimd.memset(tail_i[:, 2, :], 0).then_inc(rows_set, 1)
            link(nc.gpsimd.memset(ident[:], 0.0))
            nc.gpsimd.affine_select(out=ident[:], in_=ident[:], compare_op=ALU.not_equal, fill=1.0, base=0,
                                    pattern=[[-1, P]], channel_multiplier=1).then_inc(consts, 1)
            nc.gpsimd.iota(iota_f[:], pattern=[[1, 640]], base=0, channel_multiplier=0,
                           allow_small_or_imprecise_dtypes=True).then_inc(consts, 1)
            nc.gpsimd.memset(mhalf[:], -0.5).then_inc(consts, 1)
            nc.gpsimd.memset(ones_f[:], 1.0).then_inc(consts, 1)
            nc.gpsimd.memset(B[:], 0).then_inc(consts, 1)
            nc.gpsimd.memset(BB[:, NC * R * N:].bitcast(F32), 0.0).then_inc(consts, 1)

            def small(dst_ap, src_ap):
                pool.dma_start(dst_ap, src_ap, allow_slow_non_contiguous=True).then_inc(small_in, 16)

            for L, (a, gt) in enumerate(((att1, gate1), (att2, gate2))):
                for r in range(R):
                    small(attp[:, L, r], a[r].unsqueeze(1).broadcast_to([NB, KB]))
                    for kc in range(KC):
                        small(gw[:, L, kc, r], gt[r, :, 0].rearrange("(k c u) -> c u k", k=KB, c=KC)[kc])
            for i, v in enumerate((b0, gamma, beta)):
                small(vec0[:, i, :], v.rearrange("(c p) -> p c", p=P))
            for kc in range(KC):
                small(bias1_q[:, kc], bias1.rearrange("(k c u) -> c u k", k=KB, c=KC)[kc])

            def diff(g):
                n = min(G, T - g * G)
                if g >= 2:
                    pool.wait_ge(win_ready, g - 1)
                nc.gpsimd.tensor_tensor(
                    oh_diff[:, g % 2, 0:n * WIN].rearrange("p (t w) -> p t w", t=n),
                    iota_f[:, 0:WIN].unsqueeze(1).broadcast_to([P, n, WIN]),
                    key[:, g * G:g * G + n].unsqueeze(2).broadcast_to([P, n, WIN]),
                    ALU.subtract).then_inc(diff_ready, 1)

            pool.wait_ge(consts, 6)
            pool.wait_ge(key_ready, 1)
            diff(0)
            diff(1)
            lows = [("xT", c) for c in range(NC)] + [("w0T", k) for k in range(KC)]
            for i, (what, c) in enumerate(lows):
                pool.wait_ge(in_hi, i + 1)
                n = slice(c * PC, (c + 1) * PC)
                lo, full, hi = (xT_lo[:, :, n], xT_full[:, :, n], xT_hi[:, :, n]) if what == "xT" else \
                    (w0T_lo[:, c, :], w0T_full[:, c, :], w0T_hi[:, c, :])
                nc.gpsimd.tensor_tensor(lo, full, hi.bitcast(F32), ALU.subtract).then_inc(in_lo, 1)
                if i + 2 < NG:
                    diff(i + 2)
            for g in range(len(lows) + 2, NG):
                diff(g)
            def inverse_root(t, width, by=rstd_ready):
                nc.gpsimd.tensor_tensor(t, t, mhalf[0:t.shape[0], 0:width], ALU.pow).then_inc(by, 1)

            pool.wait_ge(deg_ready, 1)
            nc.gpsimd.tensor_tensor(dinv_p[:], deg[:], mhalf[0:PC, 0:NC], ALU.pow).then_inc(dinv_ready, 1)
            pool.wait_ge(main_full, uses[("agg0", KC - 1, 1)] + 1)
            for kc in range(KC):
                pool.dma_start(root1_raw[:, kc], root1.rearrange("(k c u) o -> c u k o", k=KB, c=KC)[kc]) \
                    .then_inc(root1_in, 16)
            pool.wait_ge(var_ready, 1)
            inverse_root(bn[:, 2, :], KC)
            for c in range(NC):
                pool.wait_ge(var_ready, 2 + c)
                inverse_root(lrs[:, c:c + 1], 1)
            pool.dma_start(bias2_b[:], bias2.unsqueeze(0).broadcast_to([PC, D])).then_inc(bias2_in, 16)
            pool.wait_ge(t_ready, NC + 2 * KC)
            for kc in range(KC):
                pool.dma_start(root2_raw[:, kc], root2.rearrange("(k c u) o -> c u k o", k=KB, c=KC)[kc]) \
                    .then_inc(root2_in, 16)
            for c in range(NC):
                pool.wait_ge(var_ready, 2 + NC + c)
                inverse_root(lrs[:, c:c + 1], 1)

        @block.tensor
        def _(pe):
            last = [None]

            def mm3(o, l_hi, l_lo, r_hi, r_lo, start, stop):
                nc.tensor.matmul(o, l_hi, r_hi, start=start, stop=False)
                nc.tensor.matmul(o, l_hi, r_lo, start=False, stop=False)
                last[0] = nc.tensor.matmul(o, l_lo, r_hi, start=False, stop=stop)

            def done():
                last[0].then_inc(main_full, 1)

            def basis(cc):
                L = cc // CH
                if cc == 0:
                    pe.wait_ge(ident_in, 2)
                if cc >= 2:
                    pe.wait_ge(w_lo, cc - 1)
                for g in range(SUB):
                    n = cc * SUB + g
                    pe.wait_ge(basis_in[n % RING], 16 * (n // RING + 1))
                    for j in range(4):
                        m = nc.tensor.matmul(psW[32 * j:32 * j + 32, cc % 2, :], S[:, L, g, :],
                                             ring[0:PB, n % RING, j, :], start=(g == 0), stop=(g == SUB - 1))
                    m.then_inc(basis_used, 1)

            pe.wait_ge(consts, 6)
            pe.wait_ge(rows_ready, 1)
            for a in range(3):
                wait_free(pe, ("edge", a))
                nc.tensor.transpose(bank(("edge", a))[:, 0:P], rows_f[:, a, :], ident[:])
                last[0] = nc.tensor.transpose(bank(("edge", a))[:, P:T], tail_f[:, a, :],
                                              ident[0:T - P, 0:T - P])
                done()
            pe.wait_ge(minmax_ready, 1)
            for i in range(2):
                nc.tensor.transpose(bank("minmax")[0:1, i * T:i * T + P], mm[:, 0, i:i + 1], ident[:])
                last[0] = nc.tensor.transpose(bank("minmax")[0:1, i * T + P:(i + 1) * T],
                                              mm[0:T - P, 1, i:i + 1], ident[0:T - P, 0:T - P])
            done()
            pe.wait_ge(x_in, 16)
            for c in range(NC):
                wait_free(pe, ("xT", c))
                for k in range(KC):
                    last[0] = nc.tensor.transpose(bank(("xT", c))[:, k * PC:(k + 1) * PC],
                                                  xs[:, c, k * P:(k + 1) * P], ident[0:PC, 0:PC])
                done()
            pe.wait_ge(base_ready, 1)
            wait_free(pe, "base")
            last[0] = nc.tensor.matmul(bank("base")[:, 0:NG], ones_f[0:1, :], gmm[0:1, 0, :], start=True, stop=True)
            done()
            pe.wait_ge(w0_in, 16)
            for k in range(KC):
                wait_free(pe, ("w0T", k))
                for o in range(KC):
                    last[0] = nc.tensor.transpose(bank(("w0T", k))[:, o * P:(o + 1) * P],
                                                  w0_raw[:, o, k * P:(k + 1) * P], ident[:])
                done()

            def xw_chunk(c):
                pe.wait_ge(in_lo, NC + KC)
                wait_free(pe, ("xw", c))
                for k in range(KC):
                    n = slice(c * PC, (c + 1) * PC)
                    mm3(bank(("xw", c))[0:PC, :], xT_hi[:, k, n], xT_lo[:, k, n], w0T_hi[:, k], w0T_lo[:, k],
                        k == 0, k == KC - 1)
                done()

            for g in range(NG):
                pe.wait_ge(win_ready, g + 1)
                if g >= 2:
                    pe.wait_ge(win_added, g - 1)
                n = min(G, T - g * G)
                for j in range(n):
                    t = g * G + j
                    pe.wait_ge(src_ready, t + 1)
                    for c in range(NC):
                        m = nc.tensor.matmul(psE[0:PC, g % 2, c * WIN:(c + 1) * WIN],
                                             oh_src[:, t % OH, c * PC:(c + 1) * PC],
                                             oh_win[:, g % 2, j * WIN:(j + 1) * WIN],
                                             start=(j == 0 and c == 0), stop=(j == n - 1 and c == NC - 1),
                                             skip_group_check=True)
                    m.then_inc(adj_used, 1)
                if g >= 12 and (g - 12) < NC:
                    xw_chunk(g - 12)
                if g % 4 == 3:
                    basis(g // 4)
            more = nc.values_load(more_i[0:1, 0:1], engines=[mybir.EngineType.PE], min_val=0, max_val=N // W)
            with pe.If(more > 0):
                with pe.Fori(0, more) as r:
                    with pe.Fori(0, T) as t:
                        pe.wait_ge(gen_ready, r * T + t + 1)
                        for c in range(NC):
                            m = nc.tensor.matmul(psE[0:PC, 0, c * WIN:(c + 1) * WIN], oh_src[:, 0, c * PC:(c + 1) * PC],
                                                 oh_win[:, 0, 0:WIN], start=(c == 0), stop=(c == NC - 1),
                                                 skip_group_check=True)
                        m.then_inc(gen_used, 1)

            pe.wait_ge(at_ready, 1)
            wait_free(pe, "deg")
            for c in range(NC):
                for s in range(NC):
                    last[0] = nc.tensor.matmul(bank("deg")[0:PC, 2 * c:2 * c + 2], AT[:, s, c * PC:(c + 1) * PC],
                                               ones_r[:, 0:2], start=(s == 0), stop=(s == NC - 1))
            done()
            basis(5)
            pe.wait_ge(diag_ready, 1)
            for h, (c0, c1) in enumerate(((0, 4), (4, NC))):
                wait_free(pe, ("dinv", h))
                for c in range(c0, c1):
                    last[0] = nc.tensor.matmul(bank(("dinv", h))[:, (c - c0) * PC:(c - c0 + 1) * PC], ones_f[0:PC, :],
                                               diag[:, c, :], start=True, stop=True)
                done()
            for f in range(KC):
                for h, (a, n) in enumerate(HALF):
                    wait_free(pe, ("agg0", f, h))
                    for s in range(NC):
                        pe.wait_ge(z_ready, s + 1)
                        for i in range(2):
                            last[0] = nc.tensor.matmul(bank(("agg0", f, h))[:, 0:n], z[:, i, s, f * P:(f + 1) * P],
                                                       AT[:, s, a:a + n], start=(s == 0 and i == 0),
                                                       stop=(s == NC - 1 and i == 1))
                    done()
            for b in range(NBB):
                wait_free(pe, ("bb", b))
                o = bank(("bb", b)).bitcast(BF16)
                for i, q in enumerate(range(4 * b, min(4 * b + 4, NC * R * NC))):
                    d, t, s = q // (R * NC), q // NC % R, q % NC
                    last[0] = nc.tensor.transpose(o[0:PC, i * P:i * P + PC],
                                                  B[:, s, t, d * PC:(d + 1) * PC].bitcast(BF16), ident16[0:PC, 0:PC])
                done()
            for c in range(NC):
                pe.wait_ge(gelu_done, KC)
                wait_free(pe, ("g", c))
                for f in range(KC):
                    last[0] = nc.tensor.transpose(bank(("g", c))[0:PC, f * P:(f + 1) * P],
                                                  hf[:, f, c * PC:(c + 1) * PC], ident[:])
                done()
            basis(6)
            for c in range(NC):
                pe.wait_ge(x1_ready, c + 1)
                wait_free(pe, ("x1T", c))
                for k in range(KC):
                    last[0] = nc.tensor.transpose(bank(("x1T", c))[:, k * PC:(k + 1) * PC],
                                                  xs[:, c, k * P:(k + 1) * P], ident[0:PC, 0:PC])
                done()
            pe.wait_ge(root_ready, KC)
            for f in range(KC):
                for h, (a, n) in enumerate(HALF):
                    wait_free(pe, ("root1", f, h))
                    if (f, h) == (0, 0):
                        pe.wait_ge(t_ready, NC)
                    for k in range(KC):
                        mm3(bank(("root1", f, h))[:, 0:n], root1_hi[:, k, f * P:(f + 1) * P], root1_lo[:, k, f * P:(f + 1) * P],
                            hlT[:, 0, k, a:a + n], hlT[:, 1, k, a:a + n], k == 0, k == KC - 1)
                    done()
            basis(7)

            def gates_and_z(L):
                wait_free(pe, ("gate", L))
                if L == 1:
                    pe.wait_ge(t_ready, NC + 2 * KC)
                for c in range(NC):
                    n = slice(c * PC, (c + 1) * PC)
                    for k in range(KC):
                        mm3(bank(("gate", L))[0:PC, 2 * c:2 * c + 2], hlT[:, 0, k, n], hlT[:, 1, k, n],
                            gw_hl[:, L, 0, k], gw_hl[:, L, 1, k], k == 0, k == KC - 1)
                done()
                for b in range(2):
                    pe.wait_ge(w_moved[b], 128 * (CH // 2) * (L + 1))
                for c in range(NC):
                    n = slice(c * PC, (c + 1) * PC)
                    for r in range(R):
                        wait_free(pe, ("Z", L, c, r))
                        for k in range(KC):
                            w = w_block(L, k)
                            mm3(bank(("Z", L, c, r))[0:PC, :], hlT[:, 0, k, n], hlT[:, 1, k, n], w[:, r, 0], w[:, r, 1],
                                k == 0, k == KC - 1)
                        done()

            gates_and_z(0)
            basis(8)
            for f in range(KC):
                for h, (a, n) in enumerate(HALF):
                    wait_free(pe, ("h", f, h))
                    for d in range(NC):
                        if f == 0 and h == 0:
                            pe.wait_ge(zg_ready, R * (d + 1))
                        for r in range(R):
                            at = (d * R + r) * N + a
                            for i in range(2):
                                last[0] = nc.tensor.matmul(bank(("h", f, h))[:, 0:n], zg[:, i, d, r, f * P:(f + 1) * P],
                                                           BB[:, at:at + n], start=(d + r + i == 0),
                                                           stop=(d == NC - 1 and r + i == 2))
                    done()
                basis(9 + f)
            for cc in range(13, 2 * CH):
                basis(cc)
            gates_and_z(1)
            for c in range(NC):
                wait_free(pe, ("out", c))
                if c == 0:
                    pe.wait_ge(root_ready, KC + 1)
                n = slice(c * PC, (c + 1) * PC)
                for k in range(KC):
                    mm3(bank(("out", c))[0:PC, :], hlT[:, 0, k, n], hlT[:, 1, k, n], root2_hi[:, k], root2_lo[:, k],
                        k == 0, False)
                for d in range(NC):
                    if c == 0:
                        pe.wait_ge(zg_ready, R * NC + R * (d + 1))
                    for r in range(R):
                        at = (d * R + r) * N + c * PC
                        for i in range(2):
                            last[0] = nc.tensor.matmul(bank(("out", c))[0:PC, :], BB[:, at:at + PC], zg[:, i, d, r, :],
                                                       start=False, stop=(d == NC - 1 and r + i == 2))
                done()

        @block.scalar
        def _(act):
            act.wait_ge(rows_set, 3)
            for a, v in enumerate((src, dst, etype)):
                act.dma_start(rows_i[:, a, :], v[0:P * P].rearrange("(t e) -> t e", e=P)).then_inc(edges_in, 16)
                act.dma_start(tail_i[0:FULL // P - P, a, :], v[P * P:FULL].rearrange("(t e) -> t e", e=P)) \
                    .then_inc(edges_in, 16)
                act.dma_start(tail_i[FULL // P - P:T - P, a, 0:E - FULL], v[FULL:E].rearrange("(t e) -> t e", t=1)) \
                    .then_inc(edges_in, 16)
            act.dma_start(xs[:], x.rearrange("(c p) o -> p c o", p=PC)).then_inc(x_in, 16)
            act.dma_start(w0_raw[:], W0.rearrange("(c p) o -> p c o", p=P)).then_inc(w0_in, 16)

            chained = [0]

            def link(ins):
                chained[0] += 1
                ins.then_inc(achain, 1)
                act.wait_ge(achain, chained[0])

            def w_part(cc):
                act.wait_ge(basis_used, SUB * (cc + 1))
                if cc >= 2:
                    act.wait_ge(w_moved[cc % 2], 128 * (cc // 2))
                hi, full = stage[:, cc % 2, 0, :], psW[:, cc % 2, :]
                if cc < CH:
                    hi, full = in_q(hi), natural(full)
                nc.scalar.activation(hi, full, ACT.Copy).then_inc(w_hi, 1)

            def window(g):
                n = min(G, T - g * G) * WIN
                act.wait_ge(diff_ready, g + 1)
                link(nc.scalar.activation(oh_diff[:, g % 2, 0:n], oh_diff[:, g % 2, 0:n], ACT.Abs))
                if g >= 2:
                    act.wait_ge(adj_used, G * (g - 1))
                nc.scalar.activation(oh_win[:, g % 2, 0:n], oh_diff[:, g % 2, 0:n], ACT.Relu,
                                     bias=ones_f[:, 0:1], scale=-1.0).then_inc(win_ready, 1)

            def parts(full, hi, ps, name):
                wait_full(act, name)
                nc.scalar.activation(hi, ps, ACT.Copy).then_inc(achain, 1)
                chained[0] += 1
                ins = nc.scalar.activation(full, ps, ACT.Copy)
                ins.then_inc(achain, 1)
                chained[0] += 1
                act.wait_ge(achain, chained[0])
                act.sem_inc(free_act, 1)
                act.sem_inc(in_hi, 1)

            act.wait_ge(consts, 6)
            for c in range(NC):
                n = slice(c * PC, (c + 1) * PC)
                parts(xT_full[:, :, n], xT_hi[:, :, n],
                      bank(("xT", c))[:, 0:KC * PC].rearrange("p (k n) -> p k n", k=KC), ("xT", c))
            window(0)
            window(1)
            for k in range(KC):
                parts(w0T_full[:, k, :], w0T_hi[:, k, :], bank(("w0T", k)), ("w0T", k))
            for g in range(NG):
                if g >= 2:
                    window(g)
                if g >= 14 and g - 14 < NC:
                    c = g - 14
                    wait_full(act, ("xw", c))
                    release(nc.scalar.activation(xw[:, c, :], bank(("xw", c))[0:PC, :], ACT.Copy), ("xw", c), "act")
                if g % 4 == 1 and g >= 5:
                    w_part(g // 4 - 1)
            w_part(4)
            act.wait_ge(free_act, releaser[:uses[("xw", NC - 1)] + 1].count("act"))
            act.wait_ge(dinv_ready, 1)
            for c in range(NC):
                nc.scalar.activation(z[:, 0, c, :], xw[:, c, :], ACT.Copy, scale=dinv_p[:, c:c + 1]).then_inc(z_hi, 1)
            w_part(5)
            act.wait_ge(z_ready, NC)
            for b in range(NBB):
                n = min(4, NC * R * NC - 4 * b)
                wait_full(act, ("bb", b))
                release(nc.scalar.activation(BB[:, 4 * b * PC:(4 * b + n) * PC].rearrange("p (b n) -> p b n", b=n),
                                             bank(("bb", b)).bitcast(U16)[0:PC, 0:n * P]
                                             .rearrange("p (b n) -> p b n", b=n)[:, :, 0:PC], ACT.Copy), ("bb", b), "act")
            for f in range(KC):
                act.wait_ge(bn_ready, 1)
                nc.scalar.activation(hf[:, f, :], hf[:, f, :], ACT.Gelu, bias=bn[:, 1, f:f + 1],
                                     scale=bn[:, 0, f:f + 1]).then_inc(gelu_done, 1)
            w_part(6)
            act.wait_ge(root1_in, 16 * KC)
            for k in range(KC):
                nc.scalar.activation(in_q(root1_hi[:, k]), natural(root1_raw[:, k]), ACT.Copy).then_inc(root_hi, 1)
            for c in range(NC):
                wait_full(act, ("x1T", c))
                nc.scalar.activation(hlT[:, 0, :, c * PC:(c + 1) * PC],
                                     bank(("x1T", c))[:, 0:KC * PC].rearrange("p (k n) -> p k n", k=KC),
                                     ACT.Copy).then_inc(t_hi, 1)
            act.wait_ge(small_in, small_total)
            for f in range(KC):
                for h, (a, n) in enumerate(HALF):
                    wait_full(act, ("root1", f, h))
                    n = min(n, N - a)
                    release(nc.scalar.activation(r1T[:, f, a:a + n], bank(("root1", f, h))[:, 0:n], ACT.Identity,
                                                 bias=bias1_q[:, f:f + 1]), ("root1", f, h), "act")
            w_part(7)

            def gates_and_z(L):
                wait_full(act, ("gate", L))
                ins = nc.scalar.activation(gate[:, L].rearrange("p c r -> p (c r)"), bank(("gate", L))[0:PC, 0:R * NC],
                                           ACT.Sigmoid)
                link(ins)
                act.sem_inc(free_act, 1)
                act.sem_inc(gate_ready, 1)
                for c in range(NC):
                    for r in range(R):
                        wait_full(act, ("Z", L, c, r))
                        nc.scalar.activation(zg[:, 0, c, r, :], bank(("Z", L, c, r))[0:PC, :], ACT.Copy,
                                             scale=gate[:, L, c, r:r + 1]).then_inc(zg_hi, 1)

            gates_and_z(0)
            w_part(8)
            for f in range(KC):
                for h, (a, n) in enumerate(HALF):
                    n = min(n, N - a)
                    act.wait_ge(h_sum, 2 * f + h + 1)
                    nc.scalar.activation(hlT[:, 0, f, a:a + n], r1T[:, f, a:a + n], ACT.Relu).then_inc(t_hi, 1)
                w_part(9 + f)
            act.wait_ge(root2_in, 16 * KC)
            nc.scalar.activation(root2_hi[:], root2_raw[:], ACT.Copy).then_inc(root_hi, 1)
            for cc in range(13, 2 * CH):
                w_part(cc)
            gates_and_z(1)

        @block.vector
        def _(dve):
            chained = [0]

            def link(ins):
                chained[0] += 1
                ins.then_inc(vchain, 1)
                dve.wait_ge(vchain, chained[0])

            v = nc.vector
            nt = T - P
            dve.wait_ge(edges_in, 16 * 9)
            v.tensor_copy(rows_f[:], rows_i[:])
            link(v.tensor_copy(tail_f[:], tail_i[:]))
            dve.sem_inc(rows_ready, 1)
            for i, op in enumerate((ALU.min, ALU.max)):
                v.tensor_reduce(mm[:, 0, i:i + 1], rows_f[:, 1, :], AX.X, op)
                last = v.tensor_reduce(mm[0:nt, 1, i:i + 1], tail_f[:, 1, :], AX.X, op)
            last.then_inc(minmax_ready, 1)
            dve.wait_ge(consts, 6)
            for a in range(3):
                wait_full(dve, ("edge", a))
                if a < 2:
                    release(v.tensor_copy(edgeT[:, a, :], bank(("edge", a))[:, 0:T]), ("edge", a), "dve")
                else:
                    release(v.tensor_scalar(edgeT[:, a, :], bank(("edge", a))[:, 0:T], 0.0, float(W), ALU.not_equal,
                                            ALU.mult), ("edge", a), "dve")
            wait_full(dve, "minmax")
            NW = T // G
            for i, op in enumerate((ALU.min, ALU.max)):
                v.tensor_reduce(gmm[0:1, i, 0:NW], bank("minmax")[0:1, i * T:i * T + NW * G]
                                .rearrange("p (g t) -> p g t", t=G), AX.X, op)
                last = v.tensor_reduce(gmm[0:1, i, NW:NG], bank("minmax")[0:1, i * T + NW * G:(i + 1) * T], AX.X, op)
            link(last)
            dve.sem_inc(free_dve, 1)
            dve.sem_inc(base_ready, 1)
            v.tensor_copy(base_i[:], gmm[0:1, 0, :])
            link(v.tensor_tensor(gmm[0:1, 2, :], gmm[0:1, 1, :], gmm[0:1, 0, :], ALU.subtract))
            link(v.tensor_reduce(gmm[0:1, 3, 0:1], gmm[0:1, 2, :], AX.X, ALU.max))
            link(v.tensor_scalar(spans[0:1, 0:13], iota_f[0:1, 1:14], float(W), gmm[0:1, 3, 0:1], ALU.mult, ALU.is_le))
            link(v.tensor_reduce(more_f[:], spans[0:1, 0:13], AX.X, ALU.add))
            link(v.tensor_copy(more_i[:], more_f[:]))
            wait_full(dve, "base")
            link(v.tensor_copy(base_b[:], bank("base")[:, 0:NG]))
            dve.sem_inc(free_dve, 1)

            def of_groups(t):
                return t[:, 0:NW * G].rearrange("p (g t) -> p g t", t=G), t[:, NW * G:T]

            (kw, kt), (dw, dt_) = of_groups(key2), of_groups(edgeT[:, 1, :])
            v.tensor_tensor(kw, dw, base_b[:, 0:NW].unsqueeze(2).broadcast_to([P, NW, G]), ALU.subtract)
            link(v.tensor_scalar(kt, dt_, base_b[:, NW:NG], None, ALU.subtract))
            link(v.tensor_scalar(key[:], key2[:], float(W), 1000.0, ALU.is_ge, ALU.mult))
            link(v.tensor_tensor(key[:], key[:], key2[:], ALU.add))
            link(v.tensor_tensor(key[:], key[:], edgeT[:, 2, :], ALU.add))
            dve.sem_inc(key_ready, 1)

            def setup():
                v.tensor_copy(ident16[:], ident[:]).then_inc(ident_in, 1)
                v.tensor_copy(ones_r[:], ones_f[0:PC, :])
                link(v.tensor_reduce(mask4[:], ident[0:PB, 0:PB].rearrange("p (b k) -> p k b", k=KB), AX.X, ALU.add))
                dve.wait_ge(small_in, small_total)
                link(v.memset(S[:], 0.0))
                for L in range(2):
                    for g in range(SUB):
                        for r in range(R):
                            last = v.tensor_scalar(S[:, L, g, 16 * r + 4 * g:16 * r + 4 * g + 4], mask4[:],
                                                   attp[:, L, r:r + 1], None, ALU.mult)
                link(v.tensor_copy(gw_hl[:, :, 0], gw[:]))
                dve.sem_inc(ident_in, 1)
                link(v.tensor_tensor(gw_hl[:, :, 1], gw[:], gw_hl[:, :, 0].bitcast(F32), ALU.subtract))

            def w_part(cc):
                dve.wait_ge(w_hi, cc + 1)
                lo, full, hi = stage[:, cc % 2, 1, :], psW[:, cc % 2, :], stage[:, cc % 2, 0, :].bitcast(F32)
                if cc < CH:
                    lo, full, hi = in_q(lo), natural(full), in_q(hi)
                v.tensor_tensor(lo, full, hi, ALU.subtract).then_inc(w_lo, 1)

            def add_window(g):
                at = nc.values_load(base_i[0:1, g:g + 1], engines=[mybir.EngineType.DVE], min_val=0, max_val=N - 1)
                dve.wait_ge(adj_used, min(T, G * (g + 1)))
                to = B[:, :, :, bass.ds(at, W)]
                link(v.tensor_tensor(to, to, psE[0:PC, g % 2, 0:NC * WIN].rearrange("p (c t w) -> p c t w", c=NC, t=R),
                                     ALU.add))
                dve.sem_inc(win_added, 1)

            for t in range(T):
                if t >= OH:
                    dve.wait_ge(adj_used, t - OH + 1)
                v.tensor_scalar(oh_src[:, t % OH, :], iota_f[:], edgeT[:, 0, t:t + 1], None, ALU.is_equal) \
                    .then_inc(src_ready, 1)
                if t == 2 * G - 1:
                    setup()
                if t % G == G // 2 and t > G:
                    add_window(t // G - 1)
                if t % (4 * G) == 2 * G - 2 and t > 4 * G:
                    w_part(t // (4 * G) - 1)
            add_window(NG - 2) if (T - 1) % G < G // 2 else None
            add_window(NG - 1)
            more = nc.values_load(more_i[0:1, 0:1], engines=[mybir.EngineType.DVE], min_val=0, max_val=N // W)
            with dve.If(more > 0):
                ROUND = 8
                v.tensor_copy(tile_f[:, 0:NW * G].rearrange("p (g t) -> p g t", t=G),
                              gmm[0:1, 0, 0:NW].unsqueeze(2).broadcast_to([1, NW, G])).then_inc(round_step, 1)
                v.tensor_copy(tile_f[:, NW * G:T], gmm[0:1, 0, NW:NG].broadcast_to([1, T - NW * G])) \
                    .then_inc(round_step, 1)
                dve.wait_ge(round_step, 2)
                with dve.Fori(0, more) as r:
                    steps = (
                        lambda: v.tensor_scalar(key2[:], key2[:], float(W), None, ALU.subtract),
                        lambda: v.tensor_scalar(key[:], key2[:], float(W), 1000.0, ALU.is_ge, ALU.mult),
                        lambda: v.tensor_scalar(beyond[:], key2[:], 0.0, 1000.0, ALU.is_lt, ALU.mult),
                        lambda: v.tensor_tensor(key[:], key[:], beyond[:], ALU.add),
                        lambda: v.tensor_tensor(key[:], key[:], key2[:], ALU.add),
                        lambda: v.tensor_tensor(key[:], key[:], edgeT[:, 2, :], ALU.add),
                        lambda: v.tensor_scalar(tile_f[:], tile_f[:], float(W), float(N - 1), ALU.add, ALU.min),
                        lambda: v.tensor_copy(tile_i[:], tile_f[:]))
                    for i, step in enumerate(steps):
                        if i:
                            dve.wait_ge(round_step, r * ROUND + i + 2)
                        step().then_inc(round_step, 1)
                    with dve.Fori(0, T) as t:
                        dve.wait_ge(round_step, (r + 1) * ROUND + 2)
                        v.tensor_scalar(oh_src[:, 0, :], iota_f[:], edgeT[:, 0, bass.ds(t, 1)], None, ALU.is_equal)
                        v.tensor_scalar(oh_win[:, 0, 0:WIN], iota_f[:, 0:WIN], key[:, bass.ds(t, 1)], None,
                                        ALU.is_equal).then_inc(gen_ready, 1)
                        at = nc.values_load(tile_i[0:1, bass.ds(t, 1)], engines=[mybir.EngineType.DVE], min_val=0,
                                            max_val=N - 1)
                        to = B[:, :, :, bass.ds(at, W)]
                        dve.wait_ge(gen_used, r * T + t + 1)
                        v.tensor_tensor(to, to, psE[0:PC, 0, 0:NC * WIN]
                                        .rearrange("p (c t w) -> p c t w", c=NC, t=R), ALU.add).then_inc(gen_added, 1)
                        dve.wait_ge(gen_added, r * T + t + 1)

            v.tensor_tensor(AT[:], B[:, :, 0, 0:N2], B[:, :, 1, 0:N2], ALU.add).then_inc(vchain, 1)
            chained[0] += 1
            dve.wait_ge(vchain, chained[0])
            for c in range(NC):
                d = AT[:, c, c * PC:(c + 1) * PC]
                last = v.tensor_tensor(d, d.bitcast(F32), ident[0:PC, 0:PC], ALU.add)
            last.then_inc(at_ready, 1)
            w_part(4)
            wait_full(dve, "deg")
            link(v.tensor_copy(deg[:], bank("deg")[0:PC, 0:2 * NC:2]))
            dve.sem_inc(free_dve, 1)
            dve.sem_inc(deg_ready, 1)
            dve.wait_ge(dinv_ready, 1)
            for c in range(NC):
                last = v.tensor_scalar(diag[:, c, :], ident[0:PC, 0:PC], dinv_p[:, c:c + 1], None, ALU.mult)
            last.then_inc(diag_ready, 1)
            for h, (c0, c1) in enumerate(((0, 4), (4, NC))):
                wait_full(dve, ("dinv", h))
                release(v.tensor_copy(dinv_b[:, c0 * PC:c1 * PC], bank(("dinv", h))[:, 0:(c1 - c0) * PC]),
                        ("dinv", h), "dve")
            for c in range(NC):
                dve.wait_ge(z_hi, c + 1)
                v.scalar_tensor_tensor(out=z[:, 1, c, :], in0=xw[:, c, :], scalar=dinv_p[:, c:c + 1],
                                       in1=z[:, 0, c, :].bitcast(F32), op0=ALU.mult, op1=ALU.subtract) \
                    .then_inc(z_ready, 1)
            w_part(5)
            for f in range(KC):
                for h, (a, n) in enumerate(HALF):
                    n = min(n, N - a)
                    wait_full(dve, ("agg0", f, h))
                    link(v.tensor_tensor(hf[:, f, a:a + n], bank(("agg0", f, h))[:, 0:n], dinv_b[:, a:a + n], ALU.mult))
                    dve.sem_inc(free_dve, 1)
                    last = v.bn_stats(bst[:, f, h, :], hf[:, f, a:a + n])
            link(last)
            for f in range(KC):
                last = v.bn_aggr(bag[:, f, :], bst[:, f].rearrange("p h s -> p (h s)"))
            link(last)
            link(v.tensor_scalar(bn[:, 2, :], bag[:, :, 1], EPS, None, ALU.add))
            dve.sem_inc(var_ready, 1)
            dve.wait_ge(rstd_ready, 1)
            v.tensor_tensor(bn[:, 0, :], bn[:, 2, :], vec0[:, 1, :], ALU.mult)
            link(v.tensor_tensor(bn[:, 3, :], bag[:, :, 0], vec0[:, 0, :], ALU.add))
            link(v.tensor_tensor(bn[:, 3, :], vec0[:, 0, :], bn[:, 3, :], ALU.subtract))
            link(v.tensor_tensor(bn[:, 3, :], bn[:, 3, :], bn[:, 0, :], ALU.mult))
            link(v.tensor_tensor(bn[:, 1, :], bn[:, 3, :], vec0[:, 2, :], ALU.add))
            dve.sem_inc(bn_ready, 1)

            def statistics(c, full):
                link(v.bn_stats(lst[:, c, :], full))
                link(v.bn_aggr(lag[:, c, :], lst[:, c, :]))
                v.tensor_scalar(lrs[:, c:c + 1], lag[:, c, 1:2], EPS, None, ALU.add).then_inc(var_ready, 1)

            def normalise(L, c, full, ready):
                dve.wait_ge(rstd_ready, 2 + L * NC + c)
                v.tensor_scalar(xs[:, c, :], full, lag[:, c, 0:1], lrs[:, c:c + 1], ALU.subtract, ALU.mult) \
                    .then_inc(ready, 1)

            for c in range(NC):
                wait_full(dve, ("g", c))
                link(v.scalar_tensor_tensor(out=in_q(x_sum[:, c, :]), in0=natural(xs[:, c, :]), scalar=2.0,
                                            in1=natural(bank(("g", c))[0:PC, :]), op0=ALU.mult, op1=ALU.add))
                dve.sem_inc(free_dve, 1)
                statistics(c, x_sum[:, c, :])
                if c:
                    normalise(0, c - 1, x_sum[:, c - 1, :], x1_ready)
            normalise(0, NC - 1, x_sum[:, NC - 1, :], x1_ready)
            w_part(6)
            dve.wait_ge(free_act, releaser[:uses[("bb", NBB - 1)] + 1].count("act"))
            v.memset(hlT[:, :, :, N:N2].bitcast(F32), 0.0)
            dve.wait_ge(root_hi, KC)
            for k in range(KC):
                v.tensor_tensor(in_q(root1_lo[:, k]), natural(root1_raw[:, k]), in_q(root1_hi[:, k].bitcast(F32)),
                                ALU.subtract).then_inc(root_ready, 1)
            for c in range(NC):
                dve.wait_ge(t_hi, c + 1)
                n = slice(c * PC, (c + 1) * PC)
                ins = v.tensor_tensor(hlT[:, 1, :, n], bank(("x1T", c))[:, 0:KC * PC].rearrange("p (k n) -> p k n", k=KC),
                                      hlT[:, 0, :, n].bitcast(F32), ALU.subtract)
                link(ins)
                dve.sem_inc(free_dve, 1)
                dve.sem_inc(t_ready, 1)
            w_part(7)

            def z_parts(L):
                dve.wait_ge(gate_ready, L + 1)
                for c in range(NC):
                    for r in range(R):
                        u = (L * NC + c) * R + r
                        dve.wait_ge(zg_hi, u + 1)
                        link(v.scalar_tensor_tensor(out=zg[:, 1, c, r, :], in0=bank(("Z", L, c, r))[0:PC, :],
                                                    scalar=gate[:, L, c, r:r + 1], in1=zg[:, 0, c, r, :].bitcast(F32),
                                                    op0=ALU.mult, op1=ALU.subtract))
                        dve.sem_inc(free_dve, 1)
                        dve.sem_inc(zg_ready, 1)

            z_parts(0)
            w_part(8)
            for f in range(KC):
                for h, (a, n) in enumerate(HALF):
                    n = min(n, N - a)
                    wait_full(dve, ("h", f, h))
                    t = r1T[:, f, a:a + n]
                    link(v.tensor_tensor(t, t, bank(("h", f, h))[:, 0:n], ALU.add))
                    dve.sem_inc(free_dve, 1)
                    dve.sem_inc(h_sum, 1)
                    dve.wait_ge(t_hi, NC + 2 * f + h + 1)
                    v.scalar_tensor_tensor(out=hlT[:, 1, f, a:a + n], in0=t, scalar=0.0,
                                           in1=hlT[:, 0, f, a:a + n].bitcast(F32), op0=ALU.max, op1=ALU.subtract) \
                        .then_inc(t_ready, 1)
                w_part(9 + f)
            dve.wait_ge(root_hi, KC + 1)
            v.tensor_tensor(root2_lo[:], root2_raw[:], root2_hi[:].bitcast(F32), ALU.subtract).then_inc(root_ready, 1)
            for cc in range(13, 2 * CH):
                w_part(cc)
            z_parts(1)
            dve.wait_ge(bias2_in, 16)
            dve.wait_ge(basis_used, 2 * CH * SUB)
            for c in range(NC):
                t = res[:, c, :].rearrange("p (k c u) -> p k c u", k=KB, c=KC)
                link(v.tensor_tensor(t, q_as_natural(xs[:, c, :]),
                                     bias2_b[:].rearrange("p (k c u) -> p k c u", k=KB, c=KC), ALU.add))
                wait_full(dve, ("out", c))
                link(v.tensor_tensor(res[:, c, :], res[:, c, :], bank(("out", c))[0:PC, :], ALU.add))
                dve.sem_inc(free_dve, 1)
                statistics(c, res[:, c, :])
                if c:
                    normalise(1, c - 1, res[:, c - 1, :], o_ready)
            normalise(1, NC - 1, res[:, NC - 1, :], o_ready)


small_total = 16 * (2 * (R + R * KC) + 3 + KC)

_INS = ["x", "src", "dst", "edge_type_2", "L0_gnn_W", "L0_gnn_b", "L0_gnn_gamma", "L0_gnn_beta",
        "L1_gnn_basis1", "L1_gnn_att1", "L1_gnn_gate_w1", "L1_gnn_root1", "L1_gnn_bias1",
        "L1_gnn_basis2", "L1_gnn_att2", "L1_gnn_gate_w2", "L1_gnn_root2", "L1_gnn_bias2"]


def kernel(**inputs):
    import concourse.bacc as _bacc
    from concourse.bass_utils import run_bass_kernel_spmd as _run

    nc = _bacc.Bacc("TRN2", target_bir_lowering=False, num_devices=1)
    arrays, args = {}, []
    for name in _INS:
        a = np.ascontiguousarray(inputs[name])
        arrays[f"in_{name}_dram"] = a
        args.append(nc.dram_tensor(f"in_{name}_dram", a.shape, mybir.dt.from_np(a.dtype), kind="ExternalInput").ap())
    out = nc.dram_tensor("out_0_dram", (N, D), F32, kind="ExternalOutput").ap()
    gnn_block(nc, *args, out)
    r = _run(nc, [arrays], core_ids=[0])
    return r.results[0]["out_0_dram"]
```

```python
from contextlib import ExitStack

import numpy as np

import concourse.bass as bass
from concourse import mybir

F32 = mybir.dt.float32
F32R = mybir.dt.float32r
F16 = mybir.dt.float16
BF16 = mybir.dt.bfloat16
U16 = mybir.dt.uint16
I32 = mybir.dt.int32
ALU = mybir.AluOpType
ACT = mybir.ActivationFunctionType
AX = mybir.AxisListType

P = 128
N = 625
D = 512
E = 20625
NB = 30
R = 2
PC = 125
NC = N // PC
KC = D // P
N2 = N + 1
HALF = ((0, 320), (320, N2 - 320))
T = -(-E // P)
G = 6
NG = T // G
W = 32
WIN = R * W
BW = N - 1 + W
ROWS = T // 2
MAXW = -(-N // W)
assert T == NG * G and T == 2 * ROWS and G % 2 == 0
KB = 4
PB = NB * KB
CH = 8
SUB = 4
RING = 4
OH = 10
WBLK = 6
EPS = 1e-5


def gnn_block(nc, x, src, dst, etype, W0, b0, gamma, beta,
              basis1, att1, gate1, root1, bias1, basis2, att2, gate2, root2, bias2, out):
    ctx = ExitStack()

    def sem(name):
        return ctx.enter_context(nc.semaphore(name))

    def sb(name, shape, dt, scope=ctx):
        return scope.enter_context(nc.sbuf_tensor(name, shape, dt))

    def share(*phases):
        def length(tensors):
            return sum(int(np.prod(shape[1:])) * (2 if dt in (F16, BF16, U16) else 4) for _, shape, dt in tensors)

        made = {}
        for i, tensors in enumerate(phases):
            scope = ctx if i == len(phases) - 1 else ExitStack()
            for name, shape, dt in tensors:
                made[name] = sb(name, shape, dt, scope)
            if scope is ctx:
                rest = max(map(length, phases)) - length(tensors)
                if rest:
                    sb(f"after_{name}", [P, -(-rest // 4)], F32)
            else:
                scope.close()
        return made

    with ctx:
        reg_r = share([("basis_ring", [P, RING, SUB, D], F32)], [("res", [PC, NC, D], F32)])
        ring, res = reg_r["basis_ring"], reg_r["res"]
        stage = sb("w_stage", [P, 2, 2, D], F32R)
        w_old = share([("oh_src", [P, OH, 640], F16), ("oh_diff", [P, 2, G * WIN], F16),
                       ("oh_win", [P, 2, G * WIN], F16)],
                      [("w45", [P, 2, R, 2, D], F32R)])
        oh_src, oh_diff, oh_win, w45 = (w_old[n] for n in ("oh_src", "oh_diff", "oh_win", "w45"))
        w03 = sb("w03", [P, 4, R, 2, D], F32R)
        reg_b = share([("w0_raw", [P, KC, D], F32), ("xw", [PC, NC, D], F32), ("rows_i", [ROWS, 3, 2, P], I32)],
                      [("BB", [PC, NC * R * N + 6], F32R)])
        w0_raw, xw, rows_i, BB = (reg_b[n] for n in ("w0_raw", "xw", "rows_i", "BB"))
        reg_x = share([("B", [PC, NC, R, BW], U16), ("edgeT", [P, 3, T], F32), ("key", [P, T], F32),
                       ("key2", [P, T], F32), ("base_b", [P, NG], F32), ("beyond", [P, T], F32)],
                      [("hlT", [P, 2, KC, N2], F32R)])
        B, edgeT, key, key2, base_b, beyond, hlT = (
            reg_x[n] for n in ("B", "edgeT", "key", "key2", "base_b", "beyond", "hlT"))
        reg_z = share([("xT_full", [P, KC, N2], F32)],
                      [("xT_lo", [P, KC, N2], F32R), ("xT_hi", [P, KC, N2], F32R)],
                      [("z", [PC, 2, NC, D], F32R), ("AT", [PC, NC, N2], F32R),
                       ("dinv_b", [P, N2], F32), ("diag", [PC, NC, PC], F32)],
                      [("root1_raw", [P, KC, D], F32), ("x_sum", [PC, NC, D], F32),
                       ("root1_lo", [P, KC, D], F32R), ("root1_hi", [P, KC, D], F32R)],
                      [("zg", [PC, 2, NC, R, D], F32R)])
        xT_full, xT_lo, xT_hi, z, AT, dinv_b, diag, root1_raw, x_sum, root1_lo, root1_hi, zg = (
            reg_z[n] for n in ("xT_full", "xT_lo", "xT_hi", "z", "AT", "dinv_b", "diag", "root1_raw", "x_sum", "root1_lo", "root1_hi", "zg"))
        reg_q = share([("w0T_full", [P, KC, D], F32)],
                      [("w0T_lo", [P, KC, D], F32R), ("w0T_hi", [P, KC, D], F32R)], [("hf", [P, KC, N], F32)],
                      [("r1T", [P, KC, N], F32)], [("root2_raw", [P, KC, D], F32)],
                      [("root2_lo", [P, KC, D], F32R), ("root2_hi", [P, KC, D], F32R)])
        w0T_full, w0T_lo, w0T_hi, hf, r1T, root2_raw, root2_lo, root2_hi = (
            reg_q[n] for n in ("w0T_full", "w0T_lo", "w0T_hi", "hf", "r1T", "root2_raw", "root2_lo", "root2_hi"))
        xs = sb("xs", [PC, NC, D], F32)
        reg_e = share([("rows_f", [ROWS, 3, 2, P], F32)], [("tile_f", [1, T], F32), ("tile_i", [1, T], I32)],
                      [("bias2_b", [PC, D], F32)], [("gate_rows", [2 * R, N2], F32)])
        rows_f, tile_f, tile_i, bias2_b, gate_rows = (
            reg_e[n] for n in ("rows_f", "tile_f", "tile_i", "bias2_b", "gate_rows"))

        ident = sb("ident", [P, P], F32)
        ident16 = sb("ident16", [P, P], BF16)
        iota_f = sb("iota_f", [P, 640], F16)
        ones_r = sb("ones_r", [PC, P], F32R)
        ones_f = sb("ones_f", [P, P], F32)
        mm = sb("mm", [ROWS, 2], F32)
        gmm = sb("gmm", [1, 4, NG], F32)
        base_i = sb("base_i", [1, NG], I32)
        spans = sb("spans", [1, MAXW], F32)
        more_f = sb("more_f", [1, 1], F32)
        more_i = sb("more_i", [1, 1], I32)
        attp = sb("attp", [PB, 2, R], F32)
        mask4 = sb("mask4", [PB, KB], F32)
        S = sb("S", [PB, 2, SUB, 32], F32)
        gw = sb("gw", [P, 2, KC, R], F32)
        gw_hl = sb("gw_hl", [P, 2, KC, 2, R], F32R)
        pair_sum = sb("pair_sum", [2 * R, R], F32)
        vec0 = sb("vec0", [P, 3, KC], F32)
        bias1_q = sb("bias1_q", [P, KC], F32)
        deg = sb("deg", [PC, NC], F32)
        mhalf = sb("mhalf", [P, NC], F32)
        dinv_p = sb("dinv_p", [PC, NC], F32)
        bst = sb("bst", [P, KC, 2, 6], F32)
        bag = sb("bag", [P, KC, 2], F32)
        bn = sb("bn", [P, 4, KC], F32)
        lst = sb("lst", [PC, NC, 6], F32)
        lag = sb("lag", [PC, NC, 2], F32)
        lrs = sb("lrs", [PC, NC], F32)
        gate = sb("gate", [PC, 2, NC, R], F32)

        psM = ctx.enter_context(nc.psum_tensor("psM", [P, 4, 512], F32))
        psE = ctx.enter_context(nc.psum_tensor("psE", [P, 2, 512], F32))
        psW = ctx.enter_context(nc.psum_tensor("psW", [P, 2, 512], F32))

        rows_set = sem("rows_set")
        edges_in, att_in = sem("edges_in"), sem("att_in")
        x_in, w0_in, small_in = sem("x_in"), sem("w0_in"), sem("small_in")
        root1_in, root2_in, bias2_in = sem("root1_in"), sem("root2_in"), sem("bias2_in")
        basis_in = [sem(f"basis_in{i}") for i in range(RING)]
        basis_used = sem("basis_used")
        w_hi, w_lo = sem("w_hi"), sem("w_lo")
        w_moved = [sem(f"w_moved{i}") for i in range(2)]
        consts = sem("consts")
        round_step, gen_ready, gen_used, gen_added = (
            sem("round_step"), sem("gen_ready"), sem("gen_used"), sem("gen_added"))
        pchain = sem("pchain")
        ident_in = sem("ident_in")
        main_full = sem("main_full")
        free_act, free_dve = sem("free_act"), sem("free_dve")
        vchain = sem("vchain")
        achain = sem("achain")
        rows_ready = sem("rows_ready")
        minmax_ready = sem("minmax_ready")
        base_ready = sem("base_ready")
        key_ready = sem("key_ready")
        diff_ready, win_ready = sem("diff_ready"), sem("win_ready")
        src_ready, adj_used = sem("src_ready"), sem("adj_used")
        win_added = sem("win_added")
        in_lo, in_hi = sem("in_lo"), sem("in_hi")
        xw_ready = sem("xw_ready")
        at_ready, dinv_ready = sem("at_ready"), sem("dinv_ready")
        z_hi, z_ready = sem("z_hi"), sem("z_ready")
        deg_ready, diag_ready = sem("deg_ready"), sem("diag_ready")
        var_ready, rstd_ready = sem("var_ready"), sem("rstd_ready")
        bn_ready, gelu_done = sem("bn_ready"), sem("gelu_done")
        bb_ready = sem("bb_ready")
        x1_ready = sem("x1_ready")
        t_hi, t_ready = sem("t_hi"), sem("t_ready")
        root_hi, root_ready = sem("root_hi"), sem("root_ready")
        r1_ready = sem("r1_ready")
        gw_ready = sem("gw_ready")
        gate_rows_ready, gate_ready = sem("gate_rows_ready"), sem("gate_ready")
        zg_hi, zg_ready = sem("zg_hi"), sem("zg_ready")
        h_sum = sem("h_sum")
        o_ready, out_done = sem("o_ready"), sem("out_done")
        x_pe = {}

        uses, releaser = {}, []

        def use(name, by):
            uses[name] = len(releaser)
            releaser.append(by)

        for a in range(3):
            use(("edge", a), "dve")
        use("minmax", "dve")
        use("base", "dve")
        turned = [("xT", 0)] + [("w0T", k) for k in range(KC)] + [("xT", c) for c in range(1, NC)]
        for name in turned:
            use(name, "act")
        for c in range(NC):
            use(("xw", c), "act")
        use("deg", "dve")
        for h in range(2):
            use(("dinv", h), "dve")
        for f in range(KC):
            for h in range(2):
                use(("agg0", f, h), "dve")
        NBB = -(-NC * R * NC // 4)
        for b in range(NBB):
            use(("bb", b), "act")
        for c in range(NC):
            use(("g", c), "dve")
        for c in range(NC):
            use(("x1T", c), "dve")
        for f in range(KC):
            for h in range(2):
                use(("root1", f, h), "act")
        for L in range(2):
            for h in range(2):
                use(("gate_rows", L, h), "act")
            for c in range(NC):
                for r in range(R):
                    use(("Z", L, c, r), "dve")
                    if (c, r) == (0, 0):
                        use(("gate", L), "act")
            if L == 0:
                for f in range(KC):
                    for h in range(2):
                        use(("h", f, h), "dve")
        for c in range(NC):
            use(("out", c), "dve")

        def bank(name):
            return psM[:, uses[name] % 4, :]

        def wait_full(eng, name):
            eng.wait_ge(main_full, uses[name] + 1)

        def release(ins, name, by):
            assert releaser[uses[name]] == by
            ins.then_inc(free_act if by == "act" else free_dve, 1)

        def wait_free(pe, name):
            before = uses[name] - 4
            if before >= 0:
                by = releaser[before]
                pe.wait_ge(free_act if by == "act" else free_dve, releaser[:before + 1].count(by))

        def natural(ap):
            return ap.rearrange("p (k c u) -> p c u k", k=KB, c=KC)

        def in_q(ap):
            return ap.rearrange("p (c u k) -> p c u k", k=KB, c=KC)

        def q_as_natural(ap):
            return ap.rearrange("p (c u k) -> p k c u", k=KB, c=KC)

        def w_block(L, kc):
            b = L * KC + kc
            return w03[:, b % WBLK] if b % WBLK < 4 else w45[:, b % WBLK - 4]

        FIRST_XW = 2
        AMONG = (3, 4)
        LEAD = 2
        FIRST_LATE = 2 * (WBLK - KC) + CH

        def edge_rows(eng, a, v):
            whole = E // (2 * P)
            eng.dma_start(rows_i[0:whole, a], v[0:whole * 2 * P].rearrange("(t h e) -> t h e", h=2, e=P)) \
                .then_inc(edges_in, 16)
            eng.dma_start(rows_i[whole:ROWS, a].rearrange("t h e -> t (h e)")[:, 0:E - whole * 2 * P],
                          v[whole * 2 * P:E].rearrange("(t e) -> t e", t=1)).then_inc(edges_in, 16)

        block = ctx.enter_context(nc.Block())

        @block.sync
        def _(sp):
            sp.wait_ge(rows_set, 3)
            edge_rows(sp, 1, dst)
            for L, a in enumerate((att1, att2)):
                for r in range(R):
                    sp.dma_start(attp[:, L, r], a[r].unsqueeze(1).broadcast_to([NB, KB]),
                                 allow_slow_non_contiguous=True).then_inc(att_in, 16)

            def load(n):
                L, c, g = n // (CH * SUB), n // SUB % CH, n % SUB
                if n >= RING:
                    sp.wait_ge(basis_used, n - RING + 1)
                rows = (basis1, basis2)[L].rearrange("b (k c j g) o -> (b k) c g j o", k=KB, c=CH, j=4, g=SUB)
                sp.dma_start(ring[0:PB, n % RING], rows[:, c, g]).then_inc(basis_in[n % RING], 16)

            def move(cc):
                L, c = cc // CH, cc % CH
                sp.wait_ge(w_lo, cc + 1)
                if L * KC + c // 2 >= WBLK:
                    sp.wait_ge(main_full, uses[("Z", 0, NC - 1, R - 1)] + 1)
                elif L * KC + c // 2 >= 4:
                    sp.wait_ge(adj_used, T)
                for r in range(R):
                    for j in range(4):
                        sp.dma_start(w_block(L, c // 2)[64 * (c % 2) + 16 * j:64 * (c % 2) + 16 * j + 16, r]
                                     .bitcast(F32),
                                     stage[32 * j + 16 * r:32 * j + 16 * r + 16, cc % 2].bitcast(F32)
                                     ).then_inc(w_moved[cc % 2], 16)

            for n in range(2 * CH * SUB):
                load(n)
                if n % SUB == SUB - 1:
                    if 0 < n // SUB <= FIRST_LATE:
                        move(n // SUB - 1)
                    elif n // SUB > FIRST_LATE + 1:
                        move(n // SUB - 2)
            move(2 * CH - 2)
            move(2 * CH - 1)
            for c in range(NC):
                sp.wait_ge(o_ready, c + 1)
                sp.dma_start(out.rearrange("(c p) o -> p c o", p=PC)[:, c], xs[:, c]).then_inc(out_done, 16)
            sp.wait_ge(out_done, 16 * NC)

        @block.gpsimd
        def _(pool):
            chained = [0]

            def link(ins):
                chained[0] += 1
                ins.then_inc(pchain, 1)
                pool.wait_ge(pchain, chained[0])

            at = E % P
            for a, value in enumerate((-1, N - 1, 0)):
                nc.gpsimd.memset(rows_i[64:ROWS, a, 1, at:], value).then_inc(rows_set, 1)
            pool.wait_ge(rows_set, 3)
            link(nc.gpsimd.memset(ident[:], 0.0))
            nc.gpsimd.affine_select(out=ident[:], in_=ident[:], compare_op=ALU.not_equal, fill=1.0, base=0,
                                    pattern=[[-1, P]], channel_multiplier=1).then_inc(consts, 1)
            nc.gpsimd.iota(iota_f[:], pattern=[[1, 640]], base=0, channel_multiplier=0,
                           allow_small_or_imprecise_dtypes=True).then_inc(consts, 1)
            nc.gpsimd.memset(mhalf[:], -0.5).then_inc(consts, 1)
            nc.gpsimd.memset(ones_f[:], 1.0).then_inc(consts, 1)
            nc.gpsimd.memset(BB[:, NC * R * N:].bitcast(F32), 0.0).then_inc(consts, 1)
            nc.gpsimd.memset(B[:], 0).then_inc(consts, 1)

            def diff(g):
                n = min(G, T - g * G)
                if g >= 2:
                    pool.wait_ge(win_ready, g - 1)
                nc.gpsimd.tensor_tensor(
                    oh_diff[:, g % 2, 0:n * WIN].rearrange("p (t w) -> p t w", t=n),
                    iota_f[:, 0:WIN].unsqueeze(1).broadcast_to([P, n, WIN]),
                    key[:, g * G:g * G + n].unsqueeze(2).broadcast_to([P, n, WIN]),
                    ALU.subtract).then_inc(diff_ready, 1)

            pool.wait_ge(consts, 6)
            pool.wait_ge(key_ready, 1)
            diff(0)
            diff(1)
            for i, (what, c) in enumerate(turned):
                pool.wait_ge(in_hi, i + 1)
                n = slice(c * PC, (c + 1) * PC)
                lo, full, hi = (xT_lo[:, :, n], xT_full[:, :, n], xT_hi[:, :, n]) if what == "xT" else \
                    (w0T_lo[:, c, :], w0T_full[:, c, :], w0T_hi[:, c, :])
                nc.gpsimd.tensor_tensor(lo, full, hi.bitcast(F32), ALU.subtract).then_inc(in_lo, 1)
                if i + 2 < NG:
                    diff(i + 2)
            for g in range(len(turned) + 2, NG):
                diff(g)

            def small(dst_ap, src_ap):
                pool.dma_start(dst_ap, src_ap, allow_slow_non_contiguous=True).then_inc(small_in, 16)

            for i, v in enumerate((b0, gamma, beta)):
                small(vec0[:, i, :], v.rearrange("(c p) -> p c", p=P))
            for kc in range(KC):
                small(bias1_q[:, kc], bias1.rearrange("(k c u) -> c u k", k=KB, c=KC)[kc])
            for L, gt in enumerate((gate1, gate2)):
                for r in range(R):
                    for kc in range(KC):
                        small(gw[:, L, kc, r], gt[r, :, 0].rearrange("(k c u) -> c u k", k=KB, c=KC)[kc])

            def inverse_root(t, width, by=rstd_ready):
                nc.gpsimd.tensor_tensor(t, t, mhalf[0:t.shape[0], 0:width], ALU.pow).then_inc(by, 1)

            pool.wait_ge(deg_ready, 1)
            nc.gpsimd.tensor_tensor(dinv_p[:], deg[:], mhalf[0:PC, 0:NC], ALU.pow).then_inc(dinv_ready, 1)
            pool.wait_ge(main_full, uses[("agg0", KC - 1, 1)] + 1)
            for kc in range(KC):
                pool.dma_start(root1_raw[:, kc], root1.rearrange("(k c u) o -> c u k o", k=KB, c=KC)[kc]) \
                    .then_inc(root1_in, 16)
            pool.wait_ge(var_ready, 1)
            inverse_root(bn[:, 2, :], KC)
            for c in range(NC):
                pool.wait_ge(var_ready, 2 + c)
                inverse_root(lrs[:, c:c + 1], 1)
            pool.wait_ge(t_ready, NC + 2 * KC)
            for kc in range(KC):
                pool.dma_start(root2_raw[:, kc], root2.rearrange("(k c u) o -> c u k o", k=KB, c=KC)[kc]) \
                    .then_inc(root2_in, 16)
            pool.wait_ge(gate_ready, 2)
            pool.dma_start(bias2_b[:], bias2.unsqueeze(0).broadcast_to([PC, D])).then_inc(bias2_in, 16)
            for c in range(NC):
                pool.wait_ge(var_ready, 2 + NC + c)
                inverse_root(lrs[:, c:c + 1], 1)

        @block.tensor
        def _(pe):
            last = [None]

            def mm3(o, l_hi, l_lo, r_hi, r_lo, start, stop):
                nc.tensor.matmul(o, l_hi, r_hi, start=start, stop=False)
                nc.tensor.matmul(o, l_hi, r_lo, start=False, stop=False)
                last[0] = nc.tensor.matmul(o, l_lo, r_hi, start=False, stop=stop)

            def done():
                last[0].then_inc(main_full, 1)

            def basis_part(n):
                cc, g = n // SUB, n % SUB
                if n == 0:
                    pe.wait_ge(ident_in, 2)
                if g == 0 and cc >= 2:
                    pe.wait_ge(w_lo, cc - 1)
                pe.wait_ge(basis_in[n % RING], 16 * (n // RING + 1))
                for j in range(4):
                    m = nc.tensor.matmul(psW[32 * j:32 * j + 32, cc % 2, :], S[:, cc // CH, g, :],
                                         ring[0:PB, n % RING, j, :], start=(g == 0), stop=(g == SUB - 1))
                m.then_inc(basis_used, 1)

            def basis(cc):
                for n in range(cc * SUB, (cc + 1) * SUB):
                    basis_part(n)

            pe.wait_ge(consts, 4)
            pe.wait_ge(rows_ready, 1)
            for a in range(3):
                wait_free(pe, ("edge", a))
                for h in range(2):
                    last[0] = nc.tensor.transpose(bank(("edge", a))[:, h * ROWS:(h + 1) * ROWS], rows_f[:, a, h, :],
                                                  ident[0:ROWS, 0:ROWS])
                done()
            pe.wait_ge(minmax_ready, 1)
            for i in range(2):
                last[0] = nc.tensor.transpose(bank("minmax")[0:1, i * ROWS:(i + 1) * ROWS], mm[:, i:i + 1],
                                              ident[0:ROWS, 0:ROWS])
            done()
            pe.wait_ge(base_ready, 1)
            wait_free(pe, "base")
            last[0] = nc.tensor.matmul(bank("base")[:, 0:NG], ones_f[0:1, :], gmm[0:1, 0, :], start=True, stop=True)
            done()
            for what, c in turned:
                pe.wait_ge(x_in if what == "xT" else w0_in, 16)
                wait_free(pe, (what, c))
                for k in range(KC):
                    if what == "xT":
                        last[0] = nc.tensor.transpose(bank(("xT", c))[:, k * PC:(k + 1) * PC],
                                                      xs[:, c, k * P:(k + 1) * P], ident[0:PC, 0:PC])
                    else:
                        last[0] = nc.tensor.transpose(bank(("w0T", c))[:, k * P:(k + 1) * P],
                                                      w0_raw[:, k, c * P:(c + 1) * P], ident[:])
                done()

            def xw_part(i):
                c, k = i // KC, i % KC
                n = slice(c * PC, (c + 1) * PC)
                pe.wait_ge(in_lo, 2 + k if c == 0 else 1 + KC + c)
                if k == 0:
                    wait_free(pe, ("xw", c))
                mm3(bank(("xw", c))[0:PC, :], xT_hi[:, k, n], xT_lo[:, k, n], w0T_hi[:, k], w0T_lo[:, k],
                    k == 0, k == KC - 1)
                if k == KC - 1:
                    done()

            basis(0)

            for g in range(NG):
                pe.wait_ge(win_ready, g + 1)
                if g >= 2:
                    pe.wait_ge(win_added, g - 1)
                n = min(G, T - g * G)
                for j in range(n):
                    t = g * G + j
                    pe.wait_ge(src_ready, t + 1)
                    for c in range(NC):
                        m = nc.tensor.matmul(psE[0:PC, g % 2, c * WIN:(c + 1) * WIN],
                                             oh_src[:, t % OH, c * PC:(c + 1) * PC],
                                             oh_win[:, g % 2, j * WIN:(j + 1) * WIN],
                                             start=(j == 0 and c == 0), stop=(j == n - 1 and c == NC - 1),
                                             skip_group_check=True)
                    m.then_inc(adj_used, 1)
                if FIRST_XW <= g < FIRST_XW + NC * KC:
                    xw_part(g - FIRST_XW)
                if g >= LEAD:
                    basis_part(SUB + g - LEAD)
            for n in range(SUB + NG - LEAD, 2 * CH * SUB // 2):
                basis_part(n)
            more = nc.values_load(more_i[0:1, 0:1], engines=[mybir.EngineType.PE], min_val=0, max_val=N // W)
            with pe.If(more > 0):
                with pe.Fori(0, more) as r:
                    with pe.Fori(0, T) as t:
                        pe.wait_ge(gen_ready, r * T + t + 1)
                        for c in range(NC):
                            m = nc.tensor.matmul(psE[0:PC, 0, c * WIN:(c + 1) * WIN], oh_src[:, 0, c * PC:(c + 1) * PC],
                                                 oh_win[:, 0, 0:WIN], start=(c == 0), stop=(c == NC - 1),
                                                 skip_group_check=True)
                        m.then_inc(gen_used, 1)

            pe.wait_ge(at_ready, 1)
            wait_free(pe, "deg")
            for c in range(NC):
                for s in range(NC):
                    last[0] = nc.tensor.matmul(bank("deg")[0:PC, 2 * c:2 * c + 2], AT[:, s, c * PC:(c + 1) * PC],
                                               ones_r[:, 0:2], start=(s == 0), stop=(s == NC - 1))
            done()
            pe.wait_ge(diag_ready, 1)
            for h, (c0, c1) in enumerate(((0, 4), (4, NC))):
                wait_free(pe, ("dinv", h))
                for c in range(c0, c1):
                    last[0] = nc.tensor.matmul(bank(("dinv", h))[:, (c - c0) * PC:(c - c0 + 1) * PC], ones_f[0:PC, :],
                                               diag[:, c, :], start=True, stop=True)
                done()
            for f in range(KC):
                for h, (a, n) in enumerate(HALF):
                    wait_free(pe, ("agg0", f, h))
                    for s in range(NC):
                        pe.wait_ge(z_ready, s + 1)
                        for i in range(2):
                            last[0] = nc.tensor.matmul(bank(("agg0", f, h))[:, 0:n], z[:, i, s, f * P:(f + 1) * P],
                                                       AT[:, s, a:a + n], start=(s == 0 and i == 0),
                                                       stop=(s == NC - 1 and i == 1))
                    done()
            for b in range(NBB):
                wait_free(pe, ("bb", b))
                o = bank(("bb", b)).bitcast(BF16)
                for i, q in enumerate(range(4 * b, min(4 * b + 4, NC * R * NC))):
                    d, t, s = q // (R * NC), q // NC % R, q % NC
                    last[0] = nc.tensor.transpose(o[0:PC, i * P:i * P + PC],
                                                  B[:, s, t, d * PC:(d + 1) * PC].bitcast(BF16), ident16[0:PC, 0:PC])
                done()
            basis(8)
            for c in range(NC):
                pe.wait_ge(gelu_done, KC)
                wait_free(pe, ("g", c))
                for f in range(KC):
                    last[0] = nc.tensor.transpose(bank(("g", c))[0:PC, f * P:(f + 1) * P],
                                                  hf[:, f, c * PC:(c + 1) * PC], ident[:])
                done()
            basis(9)
            for c in range(NC):
                pe.wait_ge(x1_ready, c + 1)
                wait_free(pe, ("x1T", c))
                for k in range(KC):
                    last[0] = nc.tensor.transpose(bank(("x1T", c))[:, k * PC:(k + 1) * PC],
                                                  xs[:, c, k * P:(k + 1) * P], ident[0:PC, 0:PC])
                done()
            pe.wait_ge(root_ready, KC)
            for f in range(KC):
                for h, (a, n) in enumerate(HALF):
                    wait_free(pe, ("root1", f, h))
                    if (f, h) == (0, 0):
                        pe.wait_ge(t_ready, NC)
                    for k in range(KC):
                        mm3(bank(("root1", f, h))[:, 0:n], root1_hi[:, k, f * P:(f + 1) * P], root1_lo[:, k, f * P:(f + 1) * P],
                            hlT[:, 0, k, a:a + n], hlT[:, 1, k, a:a + n], k == 0, k == KC - 1)
                    done()
            basis(10)

            def gates_and_z(L):
                if L == 1:
                    pe.wait_ge(t_ready, NC + 2 * KC)
                else:
                    pe.wait_ge(gw_ready, 1)
                for h, (a, n) in enumerate(HALF):
                    wait_free(pe, ("gate_rows", L, h))
                    for k in range(KC):
                        for i in range(2):
                            last[0] = nc.tensor.matmul(bank(("gate_rows", L, h))[0:2 * R, 0:n],
                                                       gw_hl[:, L, k].rearrange("p i r -> p (i r)"),
                                                       hlT[:, i, k, a:a + n], start=(k + i == 0),
                                                       stop=(k == KC - 1 and i == 1))
                    done()
                for b in range(2):
                    pe.wait_ge(w_moved[b], 128 * (CH // 2) * (L + 1))
                for c in range(NC):
                    n = slice(c * PC, (c + 1) * PC)
                    for r in range(R):
                        wait_free(pe, ("Z", L, c, r))
                        for k in range(KC):
                            w = w_block(L, k)
                            mm3(bank(("Z", L, c, r))[0:PC, :], hlT[:, 0, k, n], hlT[:, 1, k, n], w[:, r, 0], w[:, r, 1],
                                k == 0, k == KC - 1)
                        done()
                        if (c, r) == (0, 0):
                            pe.wait_ge(gate_rows_ready, 2 * (L + 1))
                            wait_free(pe, ("gate", L))
                            for d in range(NC):
                                last[0] = nc.tensor.matmul(bank(("gate", L))[0:PC, R * d:R * d + R],
                                                           gate_rows[:, d * PC:(d + 1) * PC], pair_sum[:],
                                                           start=True, stop=True)
                            done()
                    if L == 0 and c == 2:
                        basis(11)

            gates_and_z(0)
            basis(12)
            for f in range(KC):
                for h, (a, n) in enumerate(HALF):
                    wait_free(pe, ("h", f, h))
                    for d in range(NC):
                        if f == 0 and h == 0:
                            pe.wait_ge(zg_ready, R * (d + 1))
                        for r in range(R):
                            at = (d * R + r) * N + a
                            for i in range(2):
                                last[0] = nc.tensor.matmul(bank(("h", f, h))[:, 0:n], zg[:, i, d, r, f * P:(f + 1) * P],
                                                           BB[:, at:at + n], start=(d + r + i == 0),
                                                           stop=(d == NC - 1 and r + i == 2))
                    done()
                if f < 3:
                    basis(13 + f)
            gates_and_z(1)
            for c in range(NC):
                wait_free(pe, ("out", c))
                if c == 0:
                    pe.wait_ge(root_ready, KC + 1)
                n = slice(c * PC, (c + 1) * PC)
                for k in range(KC):
                    mm3(bank(("out", c))[0:PC, :], hlT[:, 0, k, n], hlT[:, 1, k, n], root2_hi[:, k], root2_lo[:, k],
                        k == 0, False)
                for d in range(NC):
                    if c == 0:
                        pe.wait_ge(zg_ready, R * NC + R * (d + 1))
                    for r in range(R):
                        at = (d * R + r) * N + c * PC
                        for i in range(2):
                            last[0] = nc.tensor.matmul(bank(("out", c))[0:PC, :], BB[:, at:at + PC], zg[:, i, d, r, :],
                                                       start=False, stop=(d == NC - 1 and r + i == 2))
                done()

        @block.scalar
        def _(act):
            act.wait_ge(rows_set, 3)
            edge_rows(act, 0, src)
            edge_rows(act, 2, etype)
            act.dma_start(xs[:], x.rearrange("(c p) o -> p c o", p=PC)).then_inc(x_in, 16)
            act.dma_start(w0_raw[:], W0.rearrange("(c p) o -> p c o", p=P)).then_inc(w0_in, 16)

            chained = [0]

            def link(ins):
                chained[0] += 1
                ins.then_inc(achain, 1)
                act.wait_ge(achain, chained[0])

            def w_part(cc):
                act.wait_ge(basis_used, SUB * (cc + 1))
                if cc >= 2:
                    act.wait_ge(w_moved[cc % 2], 128 * (cc // 2))
                hi, full = stage[:, cc % 2, 0, :], psW[:, cc % 2, :]
                if cc < CH:
                    hi, full = in_q(hi), natural(full)
                nc.scalar.activation(hi, full, ACT.Copy).then_inc(w_hi, 1)

            def window(g):
                n = min(G, T - g * G) * WIN
                act.wait_ge(diff_ready, g + 1)
                link(nc.scalar.activation(oh_diff[:, g % 2, 0:n], oh_diff[:, g % 2, 0:n], ACT.Abs))
                if g >= 2:
                    act.wait_ge(adj_used, G * (g - 1))
                nc.scalar.activation(oh_win[:, g % 2, 0:n], oh_diff[:, g % 2, 0:n], ACT.Relu,
                                     bias=ones_f[:, 0:1], scale=-1.0).then_inc(win_ready, 1)

            def parts(full, hi, ps, name):
                wait_full(act, name)
                nc.scalar.activation(hi, ps, ACT.Copy).then_inc(achain, 1)
                chained[0] += 1
                ins = nc.scalar.activation(full, ps, ACT.Copy)
                ins.then_inc(achain, 1)
                chained[0] += 1
                act.wait_ge(achain, chained[0])
                act.sem_inc(free_act, 1)
                act.sem_inc(in_hi, 1)

            act.wait_ge(consts, 4)
            for i, (what, c) in enumerate(turned):
                n = slice(c * PC, (c + 1) * PC)
                if what == "xT":
                    parts(xT_full[:, :, n], xT_hi[:, :, n],
                          bank(("xT", c))[:, 0:KC * PC].rearrange("p (k n) -> p k n", k=KC), ("xT", c))
                else:
                    parts(w0T_full[:, c, :], w0T_hi[:, c, :], bank(("w0T", c)), ("w0T", c))
                if i in AMONG:
                    window(AMONG.index(i))
            for g in range(NG):
                if g >= len(AMONG):
                    window(g)
                if g - FIRST_XW > KC and (g - FIRST_XW) % KC == 1 and (g - FIRST_XW) // KC <= NC:
                    c = (g - FIRST_XW) // KC - 1
                    wait_full(act, ("xw", c))
                    release(nc.scalar.activation(xw[:, c, :], bank(("xw", c))[0:PC, :], ACT.Copy), ("xw", c), "act")
                if g % 4 == 3:
                    w_part(g // 4)
            w_part(6)
            w_part(7)
            act.wait_ge(free_act, releaser[:uses[("xw", NC - 1)] + 1].count("act"))
            act.wait_ge(dinv_ready, 1)
            for c in range(NC):
                nc.scalar.activation(z[:, 0, c, :], xw[:, c, :], ACT.Copy, scale=dinv_p[:, c:c + 1]).then_inc(z_hi, 1)
            act.wait_ge(z_ready, NC)
            for b in range(NBB):
                n = min(4, NC * R * NC - 4 * b)
                wait_full(act, ("bb", b))
                release(nc.scalar.activation(BB[:, 4 * b * PC:(4 * b + n) * PC].rearrange("p (b n) -> p b n", b=n),
                                             bank(("bb", b)).bitcast(U16)[0:PC, 0:n * P]
                                             .rearrange("p (b n) -> p b n", b=n)[:, :, 0:PC], ACT.Copy), ("bb", b), "act")
            for f in range(KC):
                act.wait_ge(bn_ready, 1)
                nc.scalar.activation(hf[:, f, :], hf[:, f, :], ACT.Gelu, bias=bn[:, 1, f:f + 1],
                                     scale=bn[:, 0, f:f + 1]).then_inc(gelu_done, 1)
            w_part(8)
            act.wait_ge(root1_in, 16 * KC)
            for k in range(KC):
                nc.scalar.activation(in_q(root1_hi[:, k]), natural(root1_raw[:, k]), ACT.Copy).then_inc(root_hi, 1)
            w_part(9)
            for c in range(NC):
                wait_full(act, ("x1T", c))
                nc.scalar.activation(hlT[:, 0, :, c * PC:(c + 1) * PC],
                                     bank(("x1T", c))[:, 0:KC * PC].rearrange("p (k n) -> p k n", k=KC),
                                     ACT.Copy).then_inc(t_hi, 1)
            act.wait_ge(small_in, small_total)
            for f in range(KC):
                for h, (a, n) in enumerate(HALF):
                    wait_full(act, ("root1", f, h))
                    n = min(n, N - a)
                    release(nc.scalar.activation(r1T[:, f, a:a + n], bank(("root1", f, h))[:, 0:n], ACT.Identity,
                                                 bias=bias1_q[:, f:f + 1]), ("root1", f, h), "act")
            w_part(10)

            def gates_and_z(L):
                for h, (a, n) in enumerate(HALF):
                    wait_full(act, ("gate_rows", L, h))
                    ins = nc.scalar.activation(gate_rows[:, a:a + n], bank(("gate_rows", L, h))[0:2 * R, 0:n], ACT.Copy)
                    link(ins)
                    act.sem_inc(free_act, 1)
                    act.sem_inc(gate_rows_ready, 1)
                wait_full(act, ("gate", L))
                ins = nc.scalar.activation(gate[:, L].rearrange("p c r -> p (c r)"), bank(("gate", L))[0:PC, 0:R * NC],
                                           ACT.Sigmoid)
                link(ins)
                act.sem_inc(free_act, 1)
                act.sem_inc(gate_ready, 1)
                for c in range(NC):
                    for r in range(R):
                        wait_full(act, ("Z", L, c, r))
                        nc.scalar.activation(zg[:, 0, c, r, :], bank(("Z", L, c, r))[0:PC, :], ACT.Copy,
                                             scale=gate[:, L, c, r:r + 1]).then_inc(zg_hi, 1)
                    if L == 0 and c == 3:
                        w_part(11)

            gates_and_z(0)
            w_part(12)
            for f in range(KC):
                for h, (a, n) in enumerate(HALF):
                    n = min(n, N - a)
                    act.wait_ge(h_sum, 2 * f + h + 1)
                    nc.scalar.activation(hlT[:, 0, f, a:a + n], r1T[:, f, a:a + n], ACT.Relu).then_inc(t_hi, 1)
                if f < 3:
                    w_part(13 + f)
            act.wait_ge(root2_in, 16 * KC)
            nc.scalar.activation(root2_hi[:], root2_raw[:], ACT.Copy).then_inc(root_hi, 1)
            gates_and_z(1)

        @block.vector
        def _(dve):
            chained = [0]

            def link(ins):
                chained[0] += 1
                ins.then_inc(vchain, 1)
                dve.wait_ge(vchain, chained[0])

            v = nc.vector
            dve.wait_ge(consts, 4)
            v.tensor_copy(ident16[:], ident[:]).then_inc(ident_in, 1)
            v.tensor_copy(ones_r[:], ones_f[0:PC, :])
            link(v.tensor_reduce(mask4[:], ident[0:PB, 0:PB].rearrange("p (b k) -> p k b", k=KB), AX.X, ALU.add))
            v.tensor_reduce(pair_sum[:], ident[0:2 * R, 0:2 * R].rearrange("p (i r) -> p r i", r=R), AX.X, ALU.add)
            dve.wait_ge(edges_in, 16 * 6)
            link(v.tensor_copy(rows_f[:], rows_i[:]))
            dve.sem_inc(rows_ready, 1)
            for i, op in enumerate((ALU.min, ALU.max)):
                last = v.tensor_reduce(mm[:, i:i + 1], rows_f[:, 1].rearrange("t h e -> t (h e)"), AX.X, op)
            last.then_inc(minmax_ready, 1)
            dve.wait_ge(consts, 6)
            for a in range(3):
                wait_full(dve, ("edge", a))
                to, ps = (ap.rearrange(how, h=2) for ap, how in ((edgeT[:, a, :], "p (t h) -> p h t"),
                                                                 (bank(("edge", a))[:, 0:T], "p (h t) -> p h t")))
                release(v.tensor_copy(to, ps) if a < 2 else
                        v.tensor_scalar(to, ps, 0.0, float(W), ALU.not_equal, ALU.mult), ("edge", a), "dve")
            wait_full(dve, "minmax")
            for i, op in enumerate((ALU.min, ALU.max)):
                last = v.tensor_reduce(gmm[0:1, i, :], bank("minmax")[0:1, i * ROWS:(i + 1) * ROWS]
                                       .rearrange("p (g t) -> p g t", t=G // 2), AX.X, op)
            link(last)
            dve.sem_inc(free_dve, 1)
            dve.sem_inc(base_ready, 1)
            v.tensor_copy(base_i[:], gmm[0:1, 0, :])
            link(v.tensor_tensor(gmm[0:1, 2, :], gmm[0:1, 1, :], gmm[0:1, 0, :], ALU.subtract))
            link(v.tensor_reduce(gmm[0:1, 3, 0:1], gmm[0:1, 2, :], AX.X, ALU.max))
            link(v.tensor_scalar(spans[:], iota_f[0:1, 1:MAXW + 1], float(W), gmm[0:1, 3, 0:1], ALU.mult, ALU.is_le))
            link(v.tensor_reduce(more_f[:], spans[:], AX.X, ALU.add))
            link(v.tensor_copy(more_i[:], more_f[:]))
            wait_full(dve, "base")
            link(v.tensor_copy(base_b[:], bank("base")[:, 0:NG]))
            dve.sem_inc(free_dve, 1)

            link(v.tensor_tensor(key2[:].rearrange("p (g t) -> p g t", t=G),
                                 edgeT[:, 1, :].rearrange("p (g t) -> p g t", t=G),
                                 base_b[:].unsqueeze(2).broadcast_to([P, NG, G]), ALU.subtract))
            link(v.tensor_scalar(key[:], key2[:], float(W), 1000.0, ALU.is_ge, ALU.mult))
            link(v.tensor_tensor(key[:], key[:], key2[:], ALU.add))
            link(v.tensor_tensor(key[:], key[:], edgeT[:, 2, :], ALU.add))
            dve.sem_inc(key_ready, 1)
            dve.wait_ge(att_in, 16 * 2 * R)
            link(v.memset(S[:], 0.0))
            for L in range(2):
                for g in range(SUB):
                    for r in range(R):
                        last = v.tensor_scalar(S[:, L, g, 16 * r + 4 * g:16 * r + 4 * g + 4], mask4[:],
                                               attp[:, L, r:r + 1], None, ALU.mult)
            last.then_inc(ident_in, 1)

            def w_part(cc):
                dve.wait_ge(w_hi, cc + 1)
                lo, full, hi = stage[:, cc % 2, 1, :], psW[:, cc % 2, :], stage[:, cc % 2, 0, :].bitcast(F32)
                if cc < CH:
                    lo, full, hi = in_q(lo), natural(full), in_q(hi)
                v.tensor_tensor(lo, full, hi, ALU.subtract).then_inc(w_lo, 1)

            def add_window(g):
                at = nc.values_load(base_i[0:1, g:g + 1], engines=[mybir.EngineType.DVE], min_val=0, max_val=N - 1)
                dve.wait_ge(adj_used, min(T, G * (g + 1)))
                to = B[:, :, :, bass.ds(at, W)]
                link(v.tensor_tensor(to, to, psE[0:PC, g % 2, 0:NC * WIN].rearrange("p (c t w) -> p c t w", c=NC, t=R),
                                     ALU.add))
                dve.sem_inc(win_added, 1)

            for t in range(T):
                if t >= OH:
                    dve.wait_ge(adj_used, t - OH + 1)
                v.tensor_scalar(oh_src[:, t % OH, 0:N2], iota_f[:, 0:N2], edgeT[:, 0, t:t + 1], None, ALU.is_equal) \
                    .then_inc(src_ready, 1)
                if t % G == G // 2 and t > G:
                    add_window(t // G - 1)
                if t % (4 * G) == 3 * G + 2:
                    w_part(t // (4 * G))
            add_window(NG - 2) if (T - 1) % G < G // 2 else None
            add_window(NG - 1)
            more = nc.values_load(more_i[0:1, 0:1], engines=[mybir.EngineType.DVE], min_val=0, max_val=N // W)
            with dve.If(more > 0):
                ROUND = 8
                v.tensor_copy(tile_f[:].rearrange("p (g t) -> p g t", t=G),
                              gmm[0:1, 0, :].unsqueeze(2).broadcast_to([1, NG, G])).then_inc(round_step, 1)
                dve.wait_ge(round_step, 1)
                with dve.Fori(0, more) as r:
                    steps = (
                        lambda: v.tensor_scalar(key2[:], key2[:], float(W), None, ALU.subtract),
                        lambda: v.tensor_scalar(key[:], key2[:], float(W), 1000.0, ALU.is_ge, ALU.mult),
                        lambda: v.tensor_scalar(beyond[:], key2[:], 0.0, 1000.0, ALU.is_lt, ALU.mult),
                        lambda: v.tensor_tensor(key[:], key[:], beyond[:], ALU.add),
                        lambda: v.tensor_tensor(key[:], key[:], key2[:], ALU.add),
                        lambda: v.tensor_tensor(key[:], key[:], edgeT[:, 2, :], ALU.add),
                        lambda: v.tensor_scalar(tile_f[:], tile_f[:], float(W), float(N - 1), ALU.add, ALU.min),
                        lambda: v.tensor_copy(tile_i[:], tile_f[:]))
                    for i, step in enumerate(steps):
                        if i:
                            dve.wait_ge(round_step, r * ROUND + i + 1)
                        step().then_inc(round_step, 1)
                    with dve.Fori(0, T) as t:
                        dve.wait_ge(round_step, (r + 1) * ROUND + 1)
                        v.tensor_scalar(oh_src[:, 0, 0:N2], iota_f[:, 0:N2], edgeT[:, 0, bass.ds(t, 1)], None, ALU.is_equal)
                        v.tensor_scalar(oh_win[:, 0, 0:WIN], iota_f[:, 0:WIN], key[:, bass.ds(t, 1)], None,
                                        ALU.is_equal).then_inc(gen_ready, 1)
                        at = nc.values_load(tile_i[0:1, bass.ds(t, 1)], engines=[mybir.EngineType.DVE], min_val=0,
                                            max_val=N - 1)
                        to = B[:, :, :, bass.ds(at, W)]
                        dve.wait_ge(gen_used, r * T + t + 1)
                        v.tensor_tensor(to, to, psE[0:PC, 0, 0:NC * WIN]
                                        .rearrange("p (c t w) -> p c t w", c=NC, t=R), ALU.add).then_inc(gen_added, 1)
                        dve.wait_ge(gen_added, r * T + t + 1)

            v.tensor_tensor(AT[:], B[:, :, 0, 0:N2], B[:, :, 1, 0:N2], ALU.add).then_inc(vchain, 1)
            chained[0] += 1
            dve.wait_ge(vchain, chained[0])
            for c in range(NC):
                d = AT[:, c, c * PC:(c + 1) * PC]
                last = v.tensor_tensor(d, d.bitcast(F32), ident[0:PC, 0:PC], ALU.add)
            last.then_inc(at_ready, 1)
            w_part(6)
            w_part(7)
            wait_full(dve, "deg")
            link(v.tensor_copy(deg[:], bank("deg")[0:PC, 0:2 * NC:2]))
            dve.sem_inc(free_dve, 1)
            dve.sem_inc(deg_ready, 1)
            dve.wait_ge(dinv_ready, 1)
            for c in range(NC):
                last = v.tensor_scalar(diag[:, c, :], ident[0:PC, 0:PC], dinv_p[:, c:c + 1], None, ALU.mult)
            last.then_inc(diag_ready, 1)
            for h, (c0, c1) in enumerate(((0, 4), (4, NC))):
                wait_full(dve, ("dinv", h))
                release(v.tensor_copy(dinv_b[:, c0 * PC:c1 * PC], bank(("dinv", h))[:, 0:(c1 - c0) * PC]),
                        ("dinv", h), "dve")
            for c in range(NC):
                dve.wait_ge(z_hi, c + 1)
                v.scalar_tensor_tensor(out=z[:, 1, c, :], in0=xw[:, c, :], scalar=dinv_p[:, c:c + 1],
                                       in1=z[:, 0, c, :].bitcast(F32), op0=ALU.mult, op1=ALU.subtract) \
                    .then_inc(z_ready, 1)
            for f in range(KC):
                for h, (a, n) in enumerate(HALF):
                    n = min(n, N - a)
                    wait_full(dve, ("agg0", f, h))
                    link(v.tensor_tensor(hf[:, f, a:a + n], bank(("agg0", f, h))[:, 0:n], dinv_b[:, a:a + n], ALU.mult))
                    dve.sem_inc(free_dve, 1)
                    last = v.bn_stats(bst[:, f, h, :], hf[:, f, a:a + n])
            link(last)
            for f in range(KC):
                last = v.bn_aggr(bag[:, f, :], bst[:, f].rearrange("p h s -> p (h s)"))
            link(last)
            link(v.tensor_scalar(bn[:, 2, :], bag[:, :, 1], EPS, None, ALU.add))
            dve.sem_inc(var_ready, 1)
            dve.wait_ge(rstd_ready, 1)
            dve.wait_ge(small_in, small_total)
            v.tensor_tensor(bn[:, 0, :], bn[:, 2, :], vec0[:, 1, :], ALU.mult)
            link(v.tensor_tensor(bn[:, 3, :], bag[:, :, 0], vec0[:, 0, :], ALU.add))
            link(v.tensor_tensor(bn[:, 3, :], vec0[:, 0, :], bn[:, 3, :], ALU.subtract))
            link(v.tensor_tensor(bn[:, 3, :], bn[:, 3, :], bn[:, 0, :], ALU.mult))
            link(v.tensor_tensor(bn[:, 1, :], bn[:, 3, :], vec0[:, 2, :], ALU.add))
            dve.sem_inc(bn_ready, 1)

            def statistics(c, full):
                link(v.bn_stats(lst[:, c, :], full))
                link(v.bn_aggr(lag[:, c, :], lst[:, c, :]))
                v.tensor_scalar(lrs[:, c:c + 1], lag[:, c, 1:2], EPS, None, ALU.add).then_inc(var_ready, 1)

            def normalise(L, c, full, ready):
                dve.wait_ge(rstd_ready, 2 + L * NC + c)
                v.tensor_scalar(xs[:, c, :], full, lag[:, c, 0:1], lrs[:, c:c + 1], ALU.subtract, ALU.mult) \
                    .then_inc(ready, 1)

            w_part(8)
            for c in range(NC):
                wait_full(dve, ("g", c))
                link(v.scalar_tensor_tensor(out=in_q(x_sum[:, c, :]), in0=natural(xs[:, c, :]), scalar=2.0,
                                            in1=natural(bank(("g", c))[0:PC, :]), op0=ALU.mult, op1=ALU.add))
                dve.sem_inc(free_dve, 1)
                statistics(c, x_sum[:, c, :])
                if c:
                    normalise(0, c - 1, x_sum[:, c - 1, :], x1_ready)
            normalise(0, NC - 1, x_sum[:, NC - 1, :], x1_ready)
            w_part(9)
            dve.wait_ge(free_act, releaser[:uses[("bb", NBB - 1)] + 1].count("act"))
            v.memset(hlT[:, :, :, N:N2].bitcast(F32), 0.0)
            dve.wait_ge(root_hi, KC)
            for k in range(KC):
                v.tensor_tensor(in_q(root1_lo[:, k]), natural(root1_raw[:, k]), in_q(root1_hi[:, k].bitcast(F32)),
                                ALU.subtract).then_inc(root_ready, 1)
            for c in range(NC):
                dve.wait_ge(t_hi, c + 1)
                n = slice(c * PC, (c + 1) * PC)
                ins = v.tensor_tensor(hlT[:, 1, :, n], bank(("x1T", c))[:, 0:KC * PC].rearrange("p (k n) -> p k n", k=KC),
                                      hlT[:, 0, :, n].bitcast(F32), ALU.subtract)
                link(ins)
                dve.sem_inc(free_dve, 1)
                dve.sem_inc(t_ready, 1)
            link(v.tensor_copy(gw_hl[:, :, :, 0], gw[:]))
            v.tensor_tensor(gw_hl[:, :, :, 1], gw[:], gw_hl[:, :, :, 0].bitcast(F32), ALU.subtract).then_inc(gw_ready, 1)
            w_part(10)

            def z_parts(L):
                dve.wait_ge(gate_ready, L + 1)
                for c in range(NC):
                    for r in range(R):
                        u = (L * NC + c) * R + r
                        dve.wait_ge(zg_hi, u + 1)
                        link(v.scalar_tensor_tensor(out=zg[:, 1, c, r, :], in0=bank(("Z", L, c, r))[0:PC, :],
                                                    scalar=gate[:, L, c, r:r + 1], in1=zg[:, 0, c, r, :].bitcast(F32),
                                                    op0=ALU.mult, op1=ALU.subtract))
                        dve.sem_inc(free_dve, 1)
                        dve.sem_inc(zg_ready, 1)
                    if L == 0 and c == 3:
                        w_part(11)

            z_parts(0)
            w_part(12)
            for f in range(KC):
                for h, (a, n) in enumerate(HALF):
                    n = min(n, N - a)
                    wait_full(dve, ("h", f, h))
                    t = r1T[:, f, a:a + n]
                    link(v.tensor_tensor(t, t, bank(("h", f, h))[:, 0:n], ALU.add))
                    dve.sem_inc(free_dve, 1)
                    dve.sem_inc(h_sum, 1)
                    dve.wait_ge(t_hi, NC + 2 * f + h + 1)
                    v.scalar_tensor_tensor(out=hlT[:, 1, f, a:a + n], in0=t, scalar=0.0,
                                           in1=hlT[:, 0, f, a:a + n].bitcast(F32), op0=ALU.max, op1=ALU.subtract) \
                        .then_inc(t_ready, 1)
                if f < 3:
                    w_part(13 + f)
            dve.wait_ge(root_hi, KC + 1)
            v.tensor_tensor(root2_lo[:], root2_raw[:], root2_hi[:].bitcast(F32), ALU.subtract).then_inc(root_ready, 1)
            z_parts(1)
            dve.wait_ge(bias2_in, 16)
            dve.wait_ge(basis_used, 2 * CH * SUB)
            for c in range(NC):
                t = res[:, c, :].rearrange("p (k c u) -> p k c u", k=KB, c=KC)
                link(v.tensor_tensor(t, q_as_natural(xs[:, c, :]),
                                     bias2_b[:].rearrange("p (k c u) -> p k c u", k=KB, c=KC), ALU.add))
                wait_full(dve, ("out", c))
                link(v.tensor_tensor(res[:, c, :], res[:, c, :], bank(("out", c))[0:PC, :], ALU.add))
                dve.sem_inc(free_dve, 1)
                statistics(c, res[:, c, :])
                if c:
                    normalise(1, c - 1, res[:, c - 1, :], o_ready)
            normalise(1, NC - 1, res[:, NC - 1, :], o_ready)


small_total = 16 * (2 * R * KC + 3 + KC)

_INS = ["x", "src", "dst", "edge_type_2", "L0_gnn_W", "L0_gnn_b", "L0_gnn_gamma", "L0_gnn_beta",
        "L1_gnn_basis1", "L1_gnn_att1", "L1_gnn_gate_w1", "L1_gnn_root1", "L1_gnn_bias1",
        "L1_gnn_basis2", "L1_gnn_att2", "L1_gnn_gate_w2", "L1_gnn_root2", "L1_gnn_bias2"]


def kernel(**inputs):
    import concourse.bacc as _bacc
    from concourse.bass_utils import run_bass_kernel_spmd as _run

    nc = _bacc.Bacc("TRN2", target_bir_lowering=False, num_devices=1)
    arrays, args = {}, []
    for name in _INS:
        a = np.ascontiguousarray(inputs[name])
        arrays[f"in_{name}_dram"] = a
        args.append(nc.dram_tensor(f"in_{name}_dram", a.shape, mybir.dt.from_np(a.dtype), kind="ExternalInput").ap())
    out = nc.dram_tensor("out_0_dram", (N, D), F32, kind="ExternalOutput").ap()
    gnn_block(nc, *args, out)
    r = _run(nc, [arrays], core_ids=[0])
    return r.results[0]["out_0_dram"]
```

```python
from contextlib import ExitStack

import numpy as np

import concourse.bass as bass
from concourse import mybir

F32 = mybir.dt.float32
F32R = mybir.dt.float32r
F16 = mybir.dt.float16
BF16 = mybir.dt.bfloat16
U16 = mybir.dt.uint16
I32 = mybir.dt.int32
ALU = mybir.AluOpType
ACT = mybir.ActivationFunctionType
AX = mybir.AxisListType

P = 128
N = 625
D = 512
E = 20625
NB = 30
R = 2
PC = 125
NC = N // PC
KC = D // P
N2 = N + 1
HALF = ((0, 320), (320, N2 - 320))
T = -(-E // P)
G = 6
NG = T // G
W = 32
WIN = R * W
BW = N - 1 + W
ROWS = T // 2
MAXW = -(-N // W)
V_GATE, V_BIAS1, V_B, V_GAMMA, V_BETA, NV = 0, 2 * R, 2 * R + 1, 2 * R + 2, 2 * R + 3, 2 * R + 4
assert T == NG * G and T == 2 * ROWS and G % 2 == 0
KB = 4
PB = NB * KB
CH = 8
SUB = 4
RING = 4
OH = 12
GA = 4
KEYS = NC * WIN
WBLK = 6
EPS = 1e-5


def gnn_block(nc, x, src, dst, etype, W0, b0, gamma, beta,
              basis1, att1, gate1, root1, bias1, basis2, att2, gate2, root2, bias2, out):
    ctx = ExitStack()

    def sem(name):
        return ctx.enter_context(nc.semaphore(name))

    def sb(name, shape, dt, scope=ctx):
        return scope.enter_context(nc.sbuf_tensor(name, shape, dt))

    def share(*phases):
        def length(tensors):
            return sum(int(np.prod(shape[1:])) * (2 if dt in (F16, BF16, U16) else 4) for _, shape, dt in tensors)

        made = {}
        for i, tensors in enumerate(phases):
            scope = ctx if i == len(phases) - 1 else ExitStack()
            for name, shape, dt in tensors:
                made[name] = sb(name, shape, dt, scope)
            if scope is ctx:
                rest = max(map(length, phases)) - length(tensors)
                if rest:
                    sb(f"after_{name}", [P, -(-rest // 4)], F32)
            else:
                scope.close()
        return made

    with ctx:
        reg_r = share([("basis_ring", [P, RING, SUB, D], F32)], [("res", [PC, NC, D], F32)])
        ring, res = reg_r["basis_ring"], reg_r["res"]
        stage = sb("w_stage", [P, 2, 2, D], F32R)
        w_old = share([("oh_key", [P, OH, KEYS], F16), ("oh_diff", [P, 3, GA * P], F16),
                       ("oh_src", [P, 3, G * P], F16)],
                      [("before_root1_raw", [P, KC, D], F32), ("root1_raw", [P, KC, D], F32)],
                      [("w45", [P, 2, R, 2, D], F32R)])
        oh_key, oh_diff, oh_src, root1_raw, w45 = (
            w_old[n] for n in ("oh_key", "oh_diff", "oh_src", "root1_raw", "w45"))
        w03 = sb("w03", [P, 4, R, 2, D], F32R)
        reg_b = share([("w0_raw", [P, KC, D], F32), ("xw", [PC, NC, D], F32), ("rows_i", [ROWS, 3, 2, P], I32),
                       ("vec_rows", [NV, D], F32)],
                      [("BB", [PC, NC * R * N + 6], F32R)])
        w0_raw, xw, rows_i, vec_rows, BB = (reg_b[n] for n in ("w0_raw", "xw", "rows_i", "vec_rows", "BB"))
        reg_x = share([("B", [PC, NC, R, BW], U16), ("edgeT", [P, 3, T], F32), ("key", [P, T], F32),
                       ("key2", [P, T], F32), ("base_b", [P, NG], F32), ("beyond", [P, T], F32),
                       ("vec_rows_q", [NV, D], F32)],
                      [("hlT", [P, 2, KC, N2], F32R)])
        B, edgeT, key, key2, base_b, beyond, vec_rows_q, hlT = (
            reg_x[n] for n in ("B", "edgeT", "key", "key2", "base_b", "beyond", "vec_rows_q", "hlT"))
        reg_z = share([("xT_full", [P, KC, N2], F32)],
                      [("xT_lo", [P, KC, N2], F32R), ("xT_hi", [P, KC, N2], F32R)],
                      [("z", [PC, 2, NC, D], F32R), ("AT", [PC, NC, N2], F32R),
                       ("dinv_b", [P, N2], F32), ("diag", [PC, NC, PC], F32)],
                      [("x_sum", [PC, NC, D], F32),
                       ("root1_lo", [P, KC, D], F32R), ("root1_hi", [P, KC, D], F32R)],
                      [("zg", [PC, 2, NC, R, D], F32R)])
        xT_full, xT_lo, xT_hi, z, AT, dinv_b, diag, x_sum, root1_lo, root1_hi, zg = (
            reg_z[n] for n in ("xT_full", "xT_lo", "xT_hi", "z", "AT", "dinv_b", "diag", "x_sum", "root1_lo", "root1_hi", "zg"))
        reg_q = share([("w0T_full", [P, KC, D], F32)],
                      [("w0T_lo", [P, KC, D], F32R), ("w0T_hi", [P, KC, D], F32R)], [("hf", [P, KC, N], F32)],
                      [("r1T", [P, KC, N], F32)], [("root2_raw", [P, KC, D], F32)],
                      [("root2_lo", [P, KC, D], F32R), ("root2_hi", [P, KC, D], F32R)])
        w0T_full, w0T_lo, w0T_hi, hf, r1T, root2_raw, root2_lo, root2_hi = (
            reg_q[n] for n in ("w0T_full", "w0T_lo", "w0T_hi", "hf", "r1T", "root2_raw", "root2_lo", "root2_hi"))
        xs = sb("xs", [PC, NC, D], F32)
        reg_e = share([("rows_f", [ROWS, 3, 2, P], F32)], [("tile_f", [1, T], F32), ("tile_i", [1, T], I32)],
                      [("bias2_b", [PC, D], F32)], [("gate_rows", [2 * R, N2], F32)])
        rows_f, tile_f, tile_i, bias2_b, gate_rows = (
            reg_e[n] for n in ("rows_f", "tile_f", "tile_i", "bias2_b", "gate_rows"))

        ident = sb("ident", [P, P], F32)
        ident16 = sb("ident16", [P, P], BF16)
        iota_f = sb("iota_f", [P, 640], F16)
        ones_r = sb("ones_r", [PC, P], F32R)
        ones_f = sb("ones_f", [P, P], F32)
        mm = sb("mm", [ROWS, 2], F32)
        gmm = sb("gmm", [1, 4, NG], F32)
        base_i = sb("base_i", [1, NG], I32)
        spans = sb("spans", [1, MAXW], F32)
        more_f = sb("more_f", [1, 1], F32)
        more_i = sb("more_i", [1, 1], I32)
        attp = sb("attp", [PB, 2, R], F32)
        mask4 = sb("mask4", [PB, KB], F32)
        S = sb("S", [PB, 2, SUB, 32], F32)
        vecT = sb("vecT", [P, 2, KC, NV], F32)
        gw_hl = sb("gw_hl", [P, 2, KC, 2, R], F32R)
        pair_sum = sb("pair_sum", [2 * R, R], F32)
        deg = sb("deg", [PC, NC], F32)
        mhalf = sb("mhalf", [P, NC], F32)
        dinv_p = sb("dinv_p", [PC, NC], F32)
        bst = sb("bst", [P, KC, 2, 6], F32)
        bag = sb("bag", [P, KC, 2], F32)
        bn = sb("bn", [P, 4, KC], F32)
        lst = sb("lst", [PC, NC, 6], F32)
        lag = sb("lag", [PC, NC, 2], F32)
        lrs = sb("lrs", [PC, NC], F32)
        lnm = sb("lnm", [PC, 2, NC], F32)
        gate = sb("gate", [PC, 2, NC, R], F32)

        psM = ctx.enter_context(nc.psum_tensor("psM", [P, 4, 512], F32))
        psE = ctx.enter_context(nc.psum_tensor("psE", [P, 2, 512], F32))
        psW = ctx.enter_context(nc.psum_tensor("psW", [P, 2, 512], F32))

        rows_set = sem("rows_set")
        edges_in, att_in = sem("edges_in"), sem("att_in")
        x_in, w0_in, vec_in = sem("x_in"), sem("w0_in"), sem("vec_in")
        vec_permuted, vec_ready = sem("vec_permuted"), sem("vec_ready")
        root1_in, root2_in, bias2_in = sem("root1_in"), sem("root2_in"), sem("bias2_in")
        basis_in = [sem(f"basis_in{i}") for i in range(RING)]
        basis_used = sem("basis_used")
        w_hi, w_lo = sem("w_hi"), sem("w_lo")
        w_moved = [sem(f"w_moved{i}") for i in range(2)]
        consts = sem("consts")
        round_step, gen_ready, gen_used, gen_added = (
            sem("round_step"), sem("gen_ready"), sem("gen_used"), sem("gen_added"))
        pchain = sem("pchain")
        ident_in = sem("ident_in")
        main_full = sem("main_full")
        free_act, free_dve = sem("free_act"), sem("free_dve")
        vchain = sem("vchain")
        achain = sem("achain")
        rows_ready = sem("rows_ready")
        minmax_ready = sem("minmax_ready")
        base_ready = sem("base_ready")
        place_ready = sem("place_ready")
        diff_ready, src_ready = sem("diff_ready"), sem("src_ready")
        key_ready, adj_used = sem("key_ready"), sem("adj_used")
        win_added = sem("win_added")
        in_lo, in_hi = sem("in_lo"), sem("in_hi")
        xw_ready = sem("xw_ready")
        at_ready, dinv_ready = sem("at_ready"), sem("dinv_ready")
        z_hi, z_ready = sem("z_hi"), sem("z_ready")
        deg_ready, diag_ready = sem("deg_ready"), sem("diag_ready")
        var_ready, rstd_ready = sem("var_ready"), sem("rstd_ready")
        bn_ready, gelu_done = sem("bn_ready"), sem("gelu_done")
        bb_ready = sem("bb_ready")
        x1_ready = sem("x1_ready")
        t_hi, t_ready = sem("t_hi"), sem("t_ready")
        root_hi, root_ready = sem("root_hi"), sem("root_ready")
        r1_ready = sem("r1_ready")
        gw_ready = sem("gw_ready")
        gate_rows_ready, gate_ready = sem("gate_rows_ready"), sem("gate_ready")
        zg_hi, zg_ready = sem("zg_hi"), sem("zg_ready")
        h_sum = sem("h_sum")
        o_ready, out_done = sem("o_ready"), sem("out_done")
        x_pe = {}

        uses, releaser = {}, []

        def use(name, by):
            uses[name] = len(releaser)
            releaser.append(by)

        for a in range(3):
            use(("edge", a), "dve")
        use("minmax", "dve")
        use("base", "dve")
        turned = [("xT", 0)] + [("w0T", k) for k in range(KC)] + [("xT", c) for c in range(1, NC)]
        for name in turned[0:KC + 2]:
            use(name, "act")
        for c in range(NC):
            use(("xw", c), "act")
            if KC + 2 + c < len(turned):
                use(turned[KC + 2 + c], "act")
        use("vec", "act")
        use("deg", "dve")
        for h in range(2):
            use(("dinv", h), "dve")
        NBB = -(-NC * R * NC // 4)
        BB_STEPS = [[]] + [[b for b in (2 * i, 2 * i + 1) if b < NBB] for i in range(2 * KC - 1)]
        assert sum(map(len, BB_STEPS)) == NBB
        for f in range(KC):
            for h in range(2):
                use(("agg0", f, h), "dve")
                for b in BB_STEPS[2 * f + h]:
                    use(("bb", b), "act")
        for c in range(NC):
            use(("g", c), "dve")
        EARLY = -(-HALF[0][1] // PC)
        for c in range(EARLY):
            use(("x1T", c), "dve")
        for h in range(2):
            for f in range(KC):
                use(("root1", f, h), "act")
                if h == 0 and EARLY + f < NC:
                    use(("x1T", EARLY + f), "dve")
        for L in range(2):
            for h in range(2):
                use(("gate_rows", L, h), "act")
            for c in range(NC):
                for r in range(R):
                    use(("Z", L, c, r), "dve")
                    if (c, r) == (0, 0):
                        use(("gate", L), "act")
            if L == 0:
                for h in range(2):
                    for f in range(KC):
                        use(("h", f, h), "dve")
        for c in range(NC):
            use(("out", c), "dve")

        def bank(name):
            return psM[:, uses[name] % 4, :]

        def wait_full(eng, name):
            eng.wait_ge(main_full, uses[name] + 1)

        def release(ins, name, by):
            assert releaser[uses[name]] == by
            ins.then_inc(free_act if by == "act" else free_dve, 1)

        def wait_free(pe, name):
            before = uses[name] - 4
            if before >= 0:
                by = releaser[before]
                pe.wait_ge(free_act if by == "act" else free_dve, releaser[:before + 1].count(by))

        def natural(ap):
            return ap.rearrange("p (k c u) -> p c u k", k=KB, c=KC)

        def in_q(ap):
            return ap.rearrange("p (c u k) -> p c u k", k=KB, c=KC)

        def q_as_natural(ap):
            return ap.rearrange("p (c u k) -> p k c u", k=KB, c=KC)

        def w_block(L, kc):
            b = L * KC + kc
            return w03[:, b % WBLK] if b % WBLK < 4 else w45[:, b % WBLK - 4]

        FIRST_XW = 3
        TURN_FIRST = 3
        TURN_AT = dict(zip((0, 1, 4, 8, 12, 16), range(TURN_FIRST, len(turned))))
        EVICT_AT = {g + 1 + (g < 2): i for g, i in TURN_AT.items()}
        LOW_BEFORE = {2: [0], 3: [1], 4: [2], 5: [3], 6: [4]}
        for g, i in TURN_AT.items():
            if i > KC:
                LOW_BEFORE.setdefault(g + 3, []).append(i)
        LEAD = 1
        LATE_MOVES = 2 * (WBLK - KC) + CH
        MOVE_AFTER = 9

        def edge_rows(eng, a, v):
            whole = E // (2 * P)
            eng.dma_start(rows_i[0:whole, a], v[0:whole * 2 * P].rearrange("(t h e) -> t h e", h=2, e=P)) \
                .then_inc(edges_in, 16)
            eng.dma_start(rows_i[whole:ROWS, a].rearrange("t h e -> t (h e)")[:, 0:E - whole * 2 * P],
                          v[whole * 2 * P:E].rearrange("(t e) -> t e", t=1)).then_inc(edges_in, 16)

        block = ctx.enter_context(nc.Block())

        @block.sync
        def _(sp):
            sp.wait_ge(rows_set, 3)
            edge_rows(sp, 1, dst)
            for L, a in enumerate((att1, att2)):
                for r in range(R):
                    sp.dma_start(attp[:, L, r], a[r].unsqueeze(1).broadcast_to([NB, KB]),
                                 allow_slow_non_contiguous=True).then_inc(att_in, 16)

            def load(n):
                L, c, g = n // (CH * SUB), n // SUB % CH, n % SUB
                if n >= RING:
                    sp.wait_ge(basis_used, n - RING + 1)
                rows = (basis1, basis2)[L].rearrange("b (k c j g) o -> (b k) c g j o", k=KB, c=CH, j=4, g=SUB)
                sp.dma_start(ring[0:PB, n % RING], rows[:, c, g]).then_inc(basis_in[n % RING], 16)

            def move(cc, pieces=range(4 * R)):
                L, c = cc // CH, cc % CH
                if pieces[0] == 0:
                    sp.wait_ge(w_lo, cc + 1)
                    if L * KC + c // 2 >= WBLK:
                        sp.wait_ge(main_full, uses[("Z", 0, NC - 1, R - 1)] + 1)
                    elif L * KC + c // 2 == WBLK - 1:
                        sp.wait_ge(root_ready, KC)
                    elif L * KC + c // 2 >= 4:
                        sp.wait_ge(adj_used, T)
                for i in pieces:
                    r, j = i // 4, i % 4
                    sp.dma_start(w_block(L, c // 2)[64 * (c % 2) + 16 * j:64 * (c % 2) + 16 * j + 16, r]
                                 .bitcast(F32),
                                 stage[32 * j + 16 * r:32 * j + 16 * r + 16, cc % 2].bitcast(F32)
                                 ).then_inc(w_moved[cc % 2], 16)

            for n in range(2 * CH * SUB):
                load(n)
                if n == RING - 1:
                    for row, vec in ((V_GATE, gate1[:, :, 0]), (V_GATE + R, gate2[:, :, 0]), (V_BIAS1, bias1.unsqueeze(0)),
                                     (V_B, b0.unsqueeze(0)), (V_GAMMA, gamma.unsqueeze(0)), (V_BETA, beta.unsqueeze(0))):
                        sp.dma_start(vec_rows[row:row + vec.shape[0], :], vec).then_inc(vec_in, 16)
                cc, late = divmod(n - MOVE_AFTER, SUB)
                if 0 <= cc < LATE_MOVES:
                    move(cc, range(2 * late, 2 * late + 2))
            for cc in range(LATE_MOVES, 2 * CH):
                move(cc)
            for c in range(NC):
                sp.wait_ge(o_ready, c + 1)
                sp.dma_start(out.rearrange("(c p) o -> p c o", p=PC)[:, c], xs[:, c]).then_inc(out_done, 16)
            sp.wait_ge(out_done, 16 * NC)

        @block.gpsimd
        def _(pool):
            chained = [0]

            def link(ins):
                chained[0] += 1
                ins.then_inc(pchain, 1)
                pool.wait_ge(pchain, chained[0])

            at = E % P
            for a, value in enumerate((-1, N - 1, 0)):
                nc.gpsimd.memset(rows_i[64:ROWS, a, 1, at:], value).then_inc(rows_set, 1)
            pool.wait_ge(rows_set, 3)
            link(nc.gpsimd.memset(ident[:], 0.0))
            nc.gpsimd.affine_select(out=ident[:], in_=ident[:], compare_op=ALU.not_equal, fill=1.0, base=0,
                                    pattern=[[-1, P]], channel_multiplier=1).then_inc(consts, 1)
            nc.gpsimd.iota(iota_f[:], pattern=[[1, 640]], base=0, channel_multiplier=0,
                           allow_small_or_imprecise_dtypes=True).then_inc(consts, 1)
            nc.gpsimd.memset(mhalf[:], -0.5).then_inc(consts, 1)
            nc.gpsimd.memset(ones_f[:], 1.0).then_inc(consts, 1)
            nc.gpsimd.memset(BB[:, NC * R * N:].bitcast(F32), 0.0).then_inc(consts, 1)
            nc.gpsimd.memset(B[:], 0).then_inc(consts, 1)

            def diff(g):
                if g >= 3:
                    pool.wait_ge(src_ready, g - 2)
                nc.gpsimd.tensor_tensor(
                    oh_diff[:, g % 3, :].rearrange("p (t w) -> p t w", t=GA),
                    iota_f[:, 0:P].unsqueeze(1).broadcast_to([P, GA, P]),
                    edgeT[:, 0, g * G:g * G + GA].unsqueeze(2).broadcast_to([P, GA, P]),
                    ALU.subtract).then_inc(diff_ready, 1)

            pool.wait_ge(consts, 6)
            pool.wait_ge(place_ready, 1)
            diff(0)
            diff(1)
            for g in range(2, NG):
                for i in LOW_BEFORE.get(g, ()):
                    what, c = turned[i]
                    pool.wait_ge(in_hi, i + 1)
                    n = slice(c * PC, (c + 1) * PC)
                    lo, full, hi = (xT_lo[:, :, n], xT_full[:, :, n], xT_hi[:, :, n]) if what == "xT" else \
                        (w0T_lo[:, c, :], w0T_full[:, c, :], w0T_hi[:, c, :])
                    nc.gpsimd.tensor_tensor(lo, full, hi.bitcast(F32), ALU.subtract).then_inc(in_lo, 1)
                diff(g)
                if g == NG // 2:
                    pool.wait_ge(vec_in, 16 * 6)
                    nc.gpsimd.tensor_copy(in_q(vec_rows_q[:]), natural(vec_rows[:])).then_inc(vec_permuted, 1)
            def inverse_root(t, width, by=rstd_ready):
                nc.gpsimd.tensor_tensor(t, t, mhalf[0:t.shape[0], 0:width], ALU.pow).then_inc(by, 1)

            pool.wait_ge(deg_ready, 1)
            nc.gpsimd.tensor_tensor(dinv_p[:], deg[:], mhalf[0:PC, 0:NC], ALU.pow).then_inc(dinv_ready, 1)
            pool.wait_ge(at_ready, NC)
            for kc in range(KC):
                pool.dma_start(root1_raw[:, kc], root1.rearrange("(k c u) o -> c u k o", k=KB, c=KC)[kc]) \
                    .then_inc(root1_in, 16)
            for f in range(KC):
                pool.wait_ge(var_ready, f + 1)
                inverse_root(bn[:, 2, f:f + 1], 1)

            def root1_low(k):
                pool.wait_ge(root_hi, k + 1)
                nc.gpsimd.tensor_tensor(in_q(root1_lo[:, k]), natural(root1_raw[:, k]), in_q(root1_hi[:, k].bitcast(F32)),
                                        ALU.subtract).then_inc(root_ready, 1)

            for k in range(KC - 1):
                root1_low(k)
            for c in range(NC):
                pool.wait_ge(var_ready, KC + 1 + c)
                link(nc.gpsimd.tensor_tensor(lrs[:, c:c + 1], lrs[:, c:c + 1], mhalf[0:PC, 0:1], ALU.pow))
                nc.gpsimd.tensor_tensor(lnm[:, 1, c:c + 1], lnm[:, 0, c:c + 1], lrs[:, c:c + 1], ALU.mult) \
                    .then_inc(rstd_ready, 1)
                if c == 1:
                    root1_low(KC - 1)
            pool.wait_ge(t_ready, NC + 2 * KC)
            for kc in range(KC):
                pool.dma_start(root2_raw[:, kc], root2.rearrange("(k c u) o -> c u k o", k=KB, c=KC)[kc]) \
                    .then_inc(root2_in, 16)
            pool.wait_ge(gate_ready, 2)
            pool.dma_start(bias2_b[:], bias2.unsqueeze(0).broadcast_to([PC, D])).then_inc(bias2_in, 16)
            for c in range(NC):
                pool.wait_ge(var_ready, KC + NC + 1 + c)
                inverse_root(lrs[:, c:c + 1], 1)

        @block.tensor
        def _(pe):
            last = [None]

            def mm3(o, l_hi, l_lo, r_hi, r_lo, start, stop):
                nc.tensor.matmul(o, l_hi, r_hi, start=start, stop=False)
                nc.tensor.matmul(o, l_hi, r_lo, start=False, stop=False)
                last[0] = nc.tensor.matmul(o, l_lo, r_hi, start=False, stop=stop)

            def done():
                last[0].then_inc(main_full, 1)

            def basis_part(n):
                cc, g = n // SUB, n % SUB
                if n == 0:
                    pe.wait_ge(ident_in, 2)
                if g == 0 and cc >= 2:
                    pe.wait_ge(w_lo, cc - 1)
                pe.wait_ge(basis_in[n % RING], 16 * (n // RING + 1))
                for j in range(4):
                    m = nc.tensor.matmul(psW[32 * j:32 * j + 32, cc % 2, :], S[:, cc // CH, g, :],
                                         ring[0:PB, n % RING, j, :], start=(g == 0), stop=(g == SUB - 1))
                m.then_inc(basis_used, 1)

            parts_done = [0]

            def basis_upto(n):
                for i in range(parts_done[0], n + 1):
                    basis_part(i)
                parts_done[0] = n + 1

            pe.wait_ge(consts, 4)
            pe.wait_ge(rows_ready, 1)
            for a in range(3):
                wait_free(pe, ("edge", a))
                for h in range(2):
                    last[0] = nc.tensor.transpose(bank(("edge", a))[:, h * ROWS:(h + 1) * ROWS], rows_f[:, a, h, :],
                                                  ident[0:ROWS, 0:ROWS])
                done()
            pe.wait_ge(minmax_ready, 1)
            for i in range(2):
                last[0] = nc.tensor.transpose(bank("minmax")[0:1, i * ROWS:(i + 1) * ROWS], mm[:, i:i + 1],
                                              ident[0:ROWS, 0:ROWS])
            done()
            pe.wait_ge(base_ready, 1)
            wait_free(pe, "base")
            last[0] = nc.tensor.matmul(bank("base")[:, 0:NG], ones_f[0:1, :], gmm[0:1, 0, :], start=True, stop=True)
            done()
            def turn(i):
                what, c = turned[i]
                pe.wait_ge(x_in if what == "xT" else w0_in, 16)
                wait_free(pe, (what, c))
                for k in range(KC):
                    if what == "xT":
                        last[0] = nc.tensor.transpose(bank(("xT", c))[:, k * PC:(k + 1) * PC],
                                                      xs[:, c, k * P:(k + 1) * P], ident[0:PC, 0:PC])
                    else:
                        last[0] = nc.tensor.transpose(bank(("w0T", c))[:, k * P:(k + 1) * P],
                                                      w0_raw[:, k, c * P:(c + 1) * P], ident[:])
                done()

            def xw_part(i):
                c, k = i // KC, i % KC
                n = slice(c * PC, (c + 1) * PC)
                pe.wait_ge(in_lo, 2 + k if c == 0 else 1 + KC + c)
                if k == 0:
                    wait_free(pe, ("xw", c))
                mm3(bank(("xw", c))[0:PC, :], xT_hi[:, k, n], xT_lo[:, k, n], w0T_hi[:, k], w0T_lo[:, k],
                    k == 0, k == KC - 1)
                if k == KC - 1:
                    done()

            for i in range(TURN_FIRST):
                turn(i)
            for g in range(NG):
                pe.wait_ge(src_ready, g + 1)
                if g >= 2:
                    pe.wait_ge(win_added, g - 1)
                for j in range(G):
                    t = g * G + j
                    pe.wait_ge(key_ready, t + 1)
                    nc.tensor.matmul(psE[0:PC, g % 2, 0:KEYS], oh_src[:, g % 3, j * P:j * P + PC],
                                     oh_key[:, t % OH, :], start=(j == 0), stop=(j == G - 1)).then_inc(adj_used, 1)
                if g in TURN_AT:
                    turn(TURN_AT[g])
                if FIRST_XW <= g < FIRST_XW + NC * KC:
                    xw_part(g - FIRST_XW)
                basis_upto(LEAD + 4 * g // 5)
            more = nc.values_load(more_i[0:1, 0:1], engines=[mybir.EngineType.PE], min_val=0, max_val=N // W)
            with pe.If(more > 0):
                with pe.Fori(0, more) as r:
                    with pe.Fori(0, T) as t:
                        pe.wait_ge(gen_ready, r * T + t + 1)
                        nc.tensor.matmul(psE[0:PC, 0, 0:KEYS], oh_src[:, 0, 0:PC], oh_key[:, 0, :],
                                         start=True, stop=True).then_inc(gen_used, 1)

            pe.wait_ge(vec_permuted, 1)
            wait_free(pe, "vec")
            for i, rows in enumerate((vec_rows_q, vec_rows)):
                for k in range(KC):
                    at = (i * KC + k) * NV
                    last[0] = nc.tensor.transpose(bank("vec")[:, at:at + NV], rows[:, k * P:(k + 1) * P], ident[0:NV, 0:NV])
            done()
            basis_upto(24)
            wait_free(pe, "deg")
            for s in range(NC):
                pe.wait_ge(at_ready, s + 1)
                for c in range(NC):
                    last[0] = nc.tensor.matmul(bank("deg")[0:PC, 2 * c:2 * c + 2], AT[:, s, c * PC:(c + 1) * PC],
                                               ones_r[:, 0:2], start=(s == 0 and c == 0),
                                               stop=(s == NC - 1 and c == NC - 1), skip_group_check=True)
            done()
            basis_upto(25)
            pe.wait_ge(diag_ready, 1)
            for h, (c0, c1) in enumerate(((0, 4), (4, NC))):
                wait_free(pe, ("dinv", h))
                for c in range(c0, c1):
                    last[0] = nc.tensor.matmul(bank(("dinv", h))[:, (c - c0) * PC:(c - c0 + 1) * PC], ones_f[0:PC, :],
                                               diag[:, c, :], start=True, stop=True)
                done()
            basis_upto(26)
            for f in range(KC):
                for h, (a, n) in enumerate(HALF):
                    wait_free(pe, ("agg0", f, h))
                    for s in range(NC):
                        pe.wait_ge(z_ready, s + 1)
                        for i in range(2):
                            last[0] = nc.tensor.matmul(bank(("agg0", f, h))[:, 0:n], z[:, i, s, f * P:(f + 1) * P],
                                                       AT[:, s, a:a + n], start=(s == 0 and i == 0),
                                                       stop=(s == NC - 1 and i == 1))
                    done()
                    for b in BB_STEPS[2 * f + h]:
                        wait_free(pe, ("bb", b))
                        o = bank(("bb", b)).bitcast(BF16)
                        for i, q in enumerate(range(4 * b, min(4 * b + 4, NC * R * NC))):
                            d, t, s = q // (R * NC), q // NC % R, q % NC
                            last[0] = nc.tensor.transpose(o[0:PC, i * P:i * P + PC],
                                                          B[:, s, t, d * PC:(d + 1) * PC].bitcast(BF16),
                                                          ident16[0:PC, 0:PC])
                        done()
                basis_upto((28, 30, 31, 32)[f])
            basis_upto(33)
            for c in range(NC):
                pe.wait_ge(gelu_done, KC)
                wait_free(pe, ("g", c))
                for f in range(KC):
                    last[0] = nc.tensor.transpose(bank(("g", c))[0:PC, f * P:(f + 1) * P],
                                                  hf[:, f, c * PC:(c + 1) * PC], ident[:])
                done()

            def x1_turned(c):
                pe.wait_ge(x1_ready, c + 1)
                wait_free(pe, ("x1T", c))
                for k in range(KC):
                    last[0] = nc.tensor.transpose(bank(("x1T", c))[:, k * PC:(k + 1) * PC],
                                                  xs[:, c, k * P:(k + 1) * P], ident[0:PC, 0:PC])
                done()

            for c in range(EARLY):
                x1_turned(c)
                basis_upto((35, 36, 37)[c])
            pe.wait_ge(root_ready, KC)
            for h, (a, n) in enumerate(HALF):
                pe.wait_ge(t_ready, (EARLY, NC)[h])
                for f in range(KC):
                    wait_free(pe, ("root1", f, h))
                    for k in range(KC):
                        mm3(bank(("root1", f, h))[:, 0:n], root1_hi[:, k, f * P:(f + 1) * P], root1_lo[:, k, f * P:(f + 1) * P],
                            hlT[:, 0, k, a:a + n], hlT[:, 1, k, a:a + n], k == 0, k == KC - 1)
                    done()
                    if h == 0 and EARLY + f < NC:
                        x1_turned(EARLY + f)
                    basis_upto(39 + KC * h + f)

            def gates_and_z(L):
                if L == 0:
                    pe.wait_ge(gw_ready, 1)
                for h, (a, n) in enumerate(HALF):
                    if L == 1:
                        pe.wait_ge(t_ready, NC + (h + 1) * KC)
                    wait_free(pe, ("gate_rows", L, h))
                    for k in range(KC):
                        for i in range(2):
                            last[0] = nc.tensor.matmul(bank(("gate_rows", L, h))[0:2 * R, 0:n],
                                                       gw_hl[:, L, k].rearrange("p i r -> p (i r)"),
                                                       hlT[:, i, k, a:a + n], start=(k + i == 0),
                                                       stop=(k == KC - 1 and i == 1))
                    done()
                for b in range(2):
                    pe.wait_ge(w_moved[b], 128 * (CH // 2) * (L + 1))
                for c in range(NC):
                    n = slice(c * PC, (c + 1) * PC)
                    for r in range(R):
                        wait_free(pe, ("Z", L, c, r))
                        for k in range(KC):
                            w = w_block(L, k)
                            mm3(bank(("Z", L, c, r))[0:PC, :], hlT[:, 0, k, n], hlT[:, 1, k, n], w[:, r, 0], w[:, r, 1],
                                k == 0, k == KC - 1)
                        done()
                        if (c, r) == (0, 0):
                            pe.wait_ge(gate_rows_ready, 2 * (L + 1))
                            wait_free(pe, ("gate", L))
                            for d in range(NC):
                                last[0] = nc.tensor.matmul(bank(("gate", L))[0:PC, R * d:R * d + R],
                                                           gate_rows[:, d * PC:(d + 1) * PC], pair_sum[:],
                                                           start=True, stop=True)
                            done()
                        if L == 0:
                            basis_upto(47 + 7 * (R * c + r) // 5)

            gates_and_z(0)
            for h, (a, n) in enumerate(HALF):
                for f in range(KC):
                    wait_free(pe, ("h", f, h))
                    for d in range(NC):
                        if f == 0 and h == 0:
                            pe.wait_ge(zg_ready, R * (d + 1))
                        for r in range(R):
                            at = (d * R + r) * N + a
                            for i in range(2):
                                last[0] = nc.tensor.matmul(bank(("h", f, h))[:, 0:n], zg[:, i, d, r, f * P:(f + 1) * P],
                                                           BB[:, at:at + n], start=(d + r + i == 0),
                                                           stop=(d == NC - 1 and r + i == 2))
                    done()
                    basis_upto(min(60 + KC * h + f, 2 * CH * SUB - 1))
            gates_and_z(1)
            for c in range(NC):
                wait_free(pe, ("out", c))
                if c == 0:
                    pe.wait_ge(root_ready, KC + 1)
                n = slice(c * PC, (c + 1) * PC)
                for k in range(KC):
                    mm3(bank(("out", c))[0:PC, :], hlT[:, 0, k, n], hlT[:, 1, k, n], root2_hi[:, k], root2_lo[:, k],
                        k == 0, False)
                for d in range(NC):
                    if c == 0:
                        pe.wait_ge(zg_ready, R * NC + R * (d + 1))
                    for r in range(R):
                        at = (d * R + r) * N + c * PC
                        for i in range(2):
                            last[0] = nc.tensor.matmul(bank(("out", c))[0:PC, :], BB[:, at:at + PC], zg[:, i, d, r, :],
                                                       start=False, stop=(d == NC - 1 and r + i == 2))
                done()

        @block.scalar
        def _(act):
            act.wait_ge(rows_set, 3)
            edge_rows(act, 0, src)
            edge_rows(act, 2, etype)
            act.dma_start(xs[:], x.rearrange("(c p) o -> p c o", p=PC)).then_inc(x_in, 16)
            act.dma_start(w0_raw[:], W0.rearrange("(c p) o -> p c o", p=P)).then_inc(w0_in, 16)

            chained = [0]

            def link(ins):
                chained[0] += 1
                ins.then_inc(achain, 1)
                act.wait_ge(achain, chained[0])

            def w_part(cc):
                act.wait_ge(basis_used, SUB * (cc + 1))
                if cc >= 2:
                    act.wait_ge(w_moved[cc % 2], 128 * (cc // 2))
                hi, full = stage[:, cc % 2, 0, :], psW[:, cc % 2, :]
                if cc < CH:
                    hi, full = in_q(hi), natural(full)
                nc.scalar.activation(hi, full, ACT.Copy).then_inc(w_hi, 1)

            def places(g):
                act.wait_ge(diff_ready, g + 1)
                link(nc.scalar.activation(oh_diff[:, g % 3, :], oh_diff[:, g % 3, :], ACT.Abs))
                if g >= 3:
                    act.wait_ge(adj_used, G * (g - 2))
                nc.scalar.activation(oh_src[:, g % 3, 0:GA * P], oh_diff[:, g % 3, :], ACT.Relu,
                                     bias=ones_f[:, 0:1], scale=-1.0).then_inc(src_ready, 1)

            def parts(full, hi, ps, name):
                wait_full(act, name)
                nc.scalar.activation(hi, ps, ACT.Copy).then_inc(achain, 1)
                chained[0] += 1
                ins = nc.scalar.activation(full, ps, ACT.Copy)
                ins.then_inc(achain, 1)
                chained[0] += 1
                act.wait_ge(achain, chained[0])
                act.sem_inc(free_act, 1)
                act.sem_inc(in_hi, 1)

            act.wait_ge(consts, 4)
            def turned_parts(i):
                what, c = turned[i]
                n = slice(c * PC, (c + 1) * PC)
                if what == "xT":
                    parts(xT_full[:, :, n], xT_hi[:, :, n],
                          bank(("xT", c))[:, 0:KC * PC].rearrange("p (k n) -> p k n", k=KC), ("xT", c))
                else:
                    parts(w0T_full[:, c, :], w0T_hi[:, c, :], bank(("w0T", c)), ("w0T", c))

            for i in range(TURN_FIRST):
                turned_parts(i)
                if i < 2:
                    places(i)
            for g in range(NG):
                if g >= 2:
                    places(g)
                if g % 5 == 0 and g:
                    w_part(g // 5 - 1)
                if g >= FIRST_XW + KC + 1 and (g - FIRST_XW - KC - 1) % KC == 0:
                    c = (g - FIRST_XW - KC - 1) // KC
                    wait_full(act, ("xw", c))
                    release(nc.scalar.activation(xw[:, c, :], bank(("xw", c))[0:PC, :], ACT.Copy), ("xw", c), "act")
                if g in EVICT_AT:
                    turned_parts(EVICT_AT[g])
            wait_full(act, "vec")
            link(nc.scalar.activation(vecT[:].rearrange("p i k v -> p (i k v)"), bank("vec")[:, 0:2 * KC * NV], ACT.Copy))
            act.sem_inc(free_act, 1)
            act.sem_inc(vec_ready, 1)
            w_part(5)
            act.wait_ge(free_act, releaser[:uses[("xw", NC - 1)] + 1].count("act"))
            act.wait_ge(dinv_ready, 1)
            for c in range(NC):
                nc.scalar.activation(z[:, 0, c, :], xw[:, c, :], ACT.Copy, scale=dinv_p[:, c:c + 1]).then_inc(z_hi, 1)
            act.wait_ge(z_ready, NC)
            for f in range(KC + 1):
                for b in [b for step in BB_STEPS[2 * f:2 * f + 2] for b in step]:
                    n = min(4, NC * R * NC - 4 * b)
                    wait_full(act, ("bb", b))
                    release(nc.scalar.activation(BB[:, 4 * b * PC:(4 * b + n) * PC].rearrange("p (b n) -> p b n", b=n),
                                                 bank(("bb", b)).bitcast(U16)[0:PC, 0:n * P]
                                                 .rearrange("p (b n) -> p b n", b=n)[:, :, 0:PC], ACT.Copy),
                            ("bb", b), "act")
                if f == 2:
                    w_part(6)
                if f:
                    act.wait_ge(bn_ready, f)
                    nc.scalar.activation(hf[:, f - 1, :], hf[:, f - 1, :], ACT.Gelu, bias=bn[:, 1, f - 1:f],
                                         scale=bn[:, 0, f - 1:f]).then_inc(gelu_done, 1)
            act.wait_ge(root1_in, 16 * KC)
            act.wait_ge(main_full, uses[("agg0", KC - 1, 1)] + 1)
            for k in range(KC):
                nc.scalar.activation(in_q(root1_hi[:, k]), natural(root1_raw[:, k]), ACT.Copy).then_inc(root_hi, 1)
            w_part(7)

            def x1_hi(c):
                wait_full(act, ("x1T", c))
                nc.scalar.activation(hlT[:, 0, :, c * PC:(c + 1) * PC],
                                     bank(("x1T", c))[:, 0:KC * PC].rearrange("p (k n) -> p k n", k=KC),
                                     ACT.Copy).then_inc(t_hi, 1)

            act.wait_ge(free_act, releaser[:uses[("bb", NBB - 1)] + 1].count("act"))
            for c in range(NC):
                act.wait_ge(rstd_ready, KC + 1 + c)
                nc.scalar.activation(xs[:, c, :], x_sum[:, c, :], ACT.Identity, bias=lnm[:, 1, c:c + 1],
                                     scale=lrs[:, c:c + 1]).then_inc(x1_ready, 1)
                if 0 < c <= EARLY:
                    x1_hi(c - 1)
            w_part(8)
            for h, (a, n) in enumerate(HALF):
                for f in range(KC):
                    wait_full(act, ("root1", f, h))
                    n = min(n, N - a)
                    release(nc.scalar.activation(r1T[:, f, a:a + n], bank(("root1", f, h))[:, 0:n], ACT.Identity,
                                                 bias=vecT[:, 0, f, V_BIAS1:V_BIAS1 + 1]), ("root1", f, h), "act")
                    if h == 0 and EARLY + f < NC:
                        x1_hi(EARLY + f)
                    if (h, f) in ((0, 1), (1, 1)):
                        w_part(9 + h)

            def gates_and_z(L):
                for h, (a, n) in enumerate(HALF):
                    wait_full(act, ("gate_rows", L, h))
                    ins = nc.scalar.activation(gate_rows[:, a:a + n], bank(("gate_rows", L, h))[0:2 * R, 0:n], ACT.Copy)
                    link(ins)
                    act.sem_inc(free_act, 1)
                    act.sem_inc(gate_rows_ready, 1)
                wait_full(act, ("gate", L))
                ins = nc.scalar.activation(gate[:, L].rearrange("p c r -> p (c r)"), bank(("gate", L))[0:PC, 0:R * NC],
                                           ACT.Sigmoid)
                link(ins)
                act.sem_inc(free_act, 1)
                act.sem_inc(gate_ready, 1)
                for c in range(NC):
                    for r in range(R):
                        wait_full(act, ("Z", L, c, r))
                        nc.scalar.activation(zg[:, 0, c, r, :], bank(("Z", L, c, r))[0:PC, :], ACT.Copy,
                                             scale=gate[:, L, c, r:r + 1]).then_inc(zg_hi, 1)
                    if L == 0 and c in (0, 2, 4):
                        w_part(11 + c // 2)
                    if L == 1 and c == 1:
                        act.wait_ge(root2_in, 16 * KC)
                        nc.scalar.activation(root2_hi[:], root2_raw[:], ACT.Copy).then_inc(root_hi, 1)

            gates_and_z(0)
            for h, (a, n) in enumerate(HALF):
                n = min(n, N - a)
                for f in range(KC):
                    i = KC * h + f
                    act.wait_ge(h_sum, i + 1)
                    nc.scalar.activation(hlT[:, 0, f, a:a + n], r1T[:, f, a:a + n], ACT.Relu).then_inc(t_hi, 1)
                    if i in (2, 4):
                        w_part(13 + i // 2)
            gates_and_z(1)

        @block.vector
        def _(dve):
            chained = [0]

            def link(ins):
                chained[0] += 1
                ins.then_inc(vchain, 1)
                dve.wait_ge(vchain, chained[0])

            v = nc.vector
            dve.wait_ge(consts, 4)
            v.tensor_copy(ident16[:], ident[:]).then_inc(ident_in, 1)
            v.tensor_copy(ones_r[:], ones_f[0:PC, :])
            link(v.tensor_reduce(mask4[:], ident[0:PB, 0:PB].rearrange("p (b k) -> p k b", k=KB), AX.X, ALU.add))
            v.tensor_reduce(pair_sum[:], ident[0:2 * R, 0:2 * R].rearrange("p (i r) -> p r i", r=R), AX.X, ALU.add)
            dve.wait_ge(edges_in, 16 * 6)
            link(v.tensor_copy(rows_f[:], rows_i[:]))
            dve.sem_inc(rows_ready, 1)
            for i, op in enumerate((ALU.min, ALU.max)):
                last = v.tensor_reduce(mm[:, i:i + 1], rows_f[:, 1].rearrange("t h e -> t (h e)"), AX.X, op)
            last.then_inc(minmax_ready, 1)
            dve.wait_ge(consts, 6)
            for a in range(3):
                wait_full(dve, ("edge", a))
                to, ps = (ap.rearrange(how, h=2) for ap, how in ((edgeT[:, a, :], "p (t h) -> p h t"),
                                                                 (bank(("edge", a))[:, 0:T], "p (h t) -> p h t")))
                link(v.tensor_copy(to, ps) if a < 2 else
                     v.tensor_scalar(to, ps, 0.0, float(W), ALU.not_equal, ALU.mult))
                dve.sem_inc(free_dve, 1)
            chunk = beyond
            link(v.tensor_scalar(chunk[:], edgeT[:, 0, :], float(PC), None, ALU.is_ge))
            for c in range(2, NC):
                link(v.scalar_tensor_tensor(out=chunk[:], in0=edgeT[:, 0, :], scalar=float(c * PC), in1=chunk[:],
                                            op0=ALU.is_ge, op1=ALU.add))
            link(v.scalar_tensor_tensor(out=edgeT[:, 0, :], in0=chunk[:], scalar=-float(PC), in1=edgeT[:, 0, :],
                                        op0=ALU.mult, op1=ALU.add))
            dve.sem_inc(place_ready, 1)
            link(v.scalar_tensor_tensor(out=edgeT[:, 2, :], in0=chunk[:], scalar=float(WIN), in1=edgeT[:, 2, :],
                                        op0=ALU.mult, op1=ALU.add))
            wait_full(dve, "minmax")
            for i, op in enumerate((ALU.min, ALU.max)):
                last = v.tensor_reduce(gmm[0:1, i, :], bank("minmax")[0:1, i * ROWS:(i + 1) * ROWS]
                                       .rearrange("p (g t) -> p g t", t=G // 2), AX.X, op)
            link(last)
            dve.sem_inc(free_dve, 1)
            dve.sem_inc(base_ready, 1)
            v.tensor_copy(base_i[:], gmm[0:1, 0, :])
            link(v.tensor_tensor(gmm[0:1, 2, :], gmm[0:1, 1, :], gmm[0:1, 0, :], ALU.subtract))
            link(v.tensor_reduce(gmm[0:1, 3, 0:1], gmm[0:1, 2, :], AX.X, ALU.max))
            link(v.tensor_scalar(spans[:], iota_f[0:1, 1:MAXW + 1], float(W), gmm[0:1, 3, 0:1], ALU.mult, ALU.is_le))
            link(v.tensor_reduce(more_f[:], spans[:], AX.X, ALU.add))
            link(v.tensor_copy(more_i[:], more_f[:]))
            wait_full(dve, "base")
            link(v.tensor_copy(base_b[:], bank("base")[:, 0:NG]))
            dve.sem_inc(free_dve, 1)

            link(v.tensor_tensor(key2[:].rearrange("p (g t) -> p g t", t=G),
                                 edgeT[:, 1, :].rearrange("p (g t) -> p g t", t=G),
                                 base_b[:].unsqueeze(2).broadcast_to([P, NG, G]), ALU.subtract))
            link(v.tensor_scalar(key[:], key2[:], float(W), 1000.0, ALU.is_ge, ALU.mult))
            link(v.tensor_tensor(key[:], key[:], key2[:], ALU.add))
            link(v.tensor_tensor(key[:], key[:], edgeT[:, 2, :], ALU.add))
            def combine_setup():
                dve.wait_ge(att_in, 16 * 2 * R)
                link(v.memset(S[:], 0.0))
                for L in range(2):
                    for g in range(SUB):
                        for r in range(R):
                            last = v.tensor_scalar(S[:, L, g, 16 * r + 4 * g:16 * r + 4 * g + 4], mask4[:],
                                                   attp[:, L, r:r + 1], None, ALU.mult)
                last.then_inc(ident_in, 1)

            def w_part(cc):
                dve.wait_ge(w_hi, cc + 1)
                lo, full, hi = stage[:, cc % 2, 1, :], psW[:, cc % 2, :], stage[:, cc % 2, 0, :].bitcast(F32)
                if cc < CH:
                    lo, full, hi = in_q(lo), natural(full), in_q(hi)
                v.tensor_tensor(lo, full, hi, ALU.subtract).then_inc(w_lo, 1)

            def add_window(g):
                at = nc.values_load(base_i[0:1, g:g + 1], engines=[mybir.EngineType.DVE], min_val=0, max_val=N - 1)
                dve.wait_ge(adj_used, min(T, G * (g + 1)))
                to = B[:, :, :, bass.ds(at, W)]
                link(v.tensor_tensor(to, to, psE[0:PC, g % 2, 0:NC * WIN].rearrange("p (c t w) -> p c t w", c=NC, t=R),
                                     ALU.add))
                dve.sem_inc(win_added, 1)

            for t in range(T):
                if t >= OH:
                    dve.wait_ge(adj_used, t - OH + 1)
                if t % G >= GA:
                    v.tensor_scalar(oh_src[:, t // G % 3, t % G * P:(t % G + 1) * P], iota_f[:, 0:P],
                                    edgeT[:, 0, t:t + 1], None, ALU.is_equal)
                v.tensor_scalar(oh_key[:, t % OH, :], iota_f[:, 0:KEYS], key[:, t:t + 1], None, ALU.is_equal) \
                    .then_inc(key_ready, 1)
                if t == G + 1:
                    combine_setup()
                if t % G == 1 and t > 2 * G:
                    add_window(t // G - 2)
                if t % (5 * G) == 2 and t > 2:
                    w_part(t // (5 * G) - 1)
            add_window(NG - 2)
            add_window(NG - 1)
            more = nc.values_load(more_i[0:1, 0:1], engines=[mybir.EngineType.DVE], min_val=0, max_val=N // W)
            with dve.If(more > 0):
                ROUND = 8
                v.tensor_copy(tile_f[:].rearrange("p (g t) -> p g t", t=G),
                              gmm[0:1, 0, :].unsqueeze(2).broadcast_to([1, NG, G])).then_inc(round_step, 1)
                dve.wait_ge(round_step, 1)
                with dve.Fori(0, more) as r:
                    steps = (
                        lambda: v.tensor_scalar(key2[:], key2[:], float(W), None, ALU.subtract),
                        lambda: v.tensor_scalar(key[:], key2[:], float(W), 1000.0, ALU.is_ge, ALU.mult),
                        lambda: v.tensor_scalar(beyond[:], key2[:], 0.0, 1000.0, ALU.is_lt, ALU.mult),
                        lambda: v.tensor_tensor(key[:], key[:], beyond[:], ALU.add),
                        lambda: v.tensor_tensor(key[:], key[:], key2[:], ALU.add),
                        lambda: v.tensor_tensor(key[:], key[:], edgeT[:, 2, :], ALU.add),
                        lambda: v.tensor_scalar(tile_f[:], tile_f[:], float(W), float(N - 1), ALU.add, ALU.min),
                        lambda: v.tensor_copy(tile_i[:], tile_f[:]))
                    for i, step in enumerate(steps):
                        if i:
                            dve.wait_ge(round_step, r * ROUND + i + 1)
                        step().then_inc(round_step, 1)
                    with dve.Fori(0, T) as t:
                        dve.wait_ge(round_step, (r + 1) * ROUND + 1)
                        v.tensor_scalar(oh_src[:, 0, 0:P], iota_f[:, 0:P], edgeT[:, 0, bass.ds(t, 1)], None, ALU.is_equal)
                        v.tensor_scalar(oh_key[:, 0, :], iota_f[:, 0:KEYS], key[:, bass.ds(t, 1)], None,
                                        ALU.is_equal).then_inc(gen_ready, 1)
                        at = nc.values_load(tile_i[0:1, bass.ds(t, 1)], engines=[mybir.EngineType.DVE], min_val=0,
                                            max_val=N - 1)
                        to = B[:, :, :, bass.ds(at, W)]
                        dve.wait_ge(gen_used, r * T + t + 1)
                        v.tensor_tensor(to, to, psE[0:PC, 0, 0:NC * WIN]
                                        .rearrange("p (c t w) -> p c t w", c=NC, t=R), ALU.add).then_inc(gen_added, 1)
                        dve.wait_ge(gen_added, r * T + t + 1)

            for c in range(NC):
                link(v.tensor_tensor(AT[:, c], B[:, c, 0, 0:N2], B[:, c, 1, 0:N2], ALU.add))
                d = AT[:, c, c * PC:(c + 1) * PC]
                v.tensor_tensor(d, d.bitcast(F32), ident[0:PC, 0:PC], ALU.add).then_inc(at_ready, 1)
            w_part(5)
            wait_full(dve, "deg")
            link(v.tensor_copy(deg[:], bank("deg")[0:PC, 0:2 * NC:2]))
            dve.sem_inc(free_dve, 1)
            dve.sem_inc(deg_ready, 1)
            dve.wait_ge(dinv_ready, 1)
            for c in range(NC):
                last = v.tensor_scalar(diag[:, c, :], ident[0:PC, 0:PC], dinv_p[:, c:c + 1], None, ALU.mult)
            last.then_inc(diag_ready, 1)
            for c in range(NC):
                dve.wait_ge(z_hi, c + 1)
                v.scalar_tensor_tensor(out=z[:, 1, c, :], in0=xw[:, c, :], scalar=dinv_p[:, c:c + 1],
                                       in1=z[:, 0, c, :].bitcast(F32), op0=ALU.mult, op1=ALU.subtract) \
                    .then_inc(z_ready, 1)
            for h, (c0, c1) in enumerate(((0, 4), (4, NC))):
                wait_full(dve, ("dinv", h))
                link(v.tensor_copy(dinv_b[:, c0 * PC:c1 * PC], bank(("dinv", h))[:, 0:(c1 - c0) * PC]))
                dve.sem_inc(free_dve, 1)

            def bn_finish(f):
                e = slice(f, f + 1)
                dve.wait_ge(rstd_ready, f + 1)
                link(v.tensor_tensor(bn[:, 0, e], bn[:, 2, e], vecT[:, 1, f, V_GAMMA:V_GAMMA + 1], ALU.mult))
                link(v.tensor_tensor(bn[:, 3, e], bn[:, 3, e], bn[:, 0, e], ALU.mult))
                v.tensor_tensor(bn[:, 1, e], bn[:, 3, e], vecT[:, 1, f, V_BETA:V_BETA + 1], ALU.add).then_inc(bn_ready, 1)

            for f in range(KC):
                e = slice(f, f + 1)
                for h, (a, n) in enumerate(HALF):
                    n = min(n, N - a)
                    wait_full(dve, ("agg0", f, h))
                    link(v.tensor_tensor(hf[:, f, a:a + n], bank(("agg0", f, h))[:, 0:n], dinv_b[:, a:a + n], ALU.mult))
                    dve.sem_inc(free_dve, 1)
                    last = v.bn_stats(bst[:, f, h, :], hf[:, f, a:a + n])
                    if h == 0 and f:
                        bn_finish(f - 1)
                if f == 2:
                    w_part(6)
                link(last)
                link(v.bn_aggr(bag[:, f, :], bst[:, f].rearrange("p h s -> p (h s)")))
                v.tensor_scalar(bn[:, 2, e], bag[:, f, 1:2], EPS, None, ALU.add).then_inc(var_ready, 1)
                if f == 0:
                    dve.wait_ge(vec_ready, 1)
                link(v.tensor_tensor(bn[:, 3, e], bag[:, f, 0:1], vecT[:, 1, f, V_B:V_B + 1], ALU.add))
                link(v.tensor_tensor(bn[:, 3, e], vecT[:, 1, f, V_B:V_B + 1], bn[:, 3, e], ALU.subtract))
            bn_finish(KC - 1)

            def statistics(c, full):
                link(v.bn_stats(lst[:, c, :], full))
                link(v.bn_aggr(lag[:, c, :], lst[:, c, :]))

            def variance(c):
                v.tensor_scalar(lrs[:, c:c + 1], lag[:, c, 1:2], EPS, None, ALU.add).then_inc(var_ready, 1)

            def normalise(c, full, ready):
                dve.wait_ge(rstd_ready, KC + NC + 1 + c)
                v.tensor_scalar(xs[:, c, :], full, lag[:, c, 0:1], lrs[:, c:c + 1], ALU.subtract, ALU.mult) \
                    .then_inc(ready, 1)

            def residual_sum(c):
                wait_full(dve, ("g", c))
                link(v.scalar_tensor_tensor(out=in_q(x_sum[:, c, :]), in0=natural(xs[:, c, :]), scalar=2.0,
                                            in1=natural(bank(("g", c))[0:PC, :]), op0=ALU.mult, op1=ALU.add))
                dve.sem_inc(free_dve, 1)

            residual_sum(0)
            for c in range(NC):
                v.bn_stats(lst[:, c, :], x_sum[:, c, :]).then_inc(vchain, 1)
                chained[0] += 1
                if c + 1 < NC:
                    residual_sum(c + 1)
                else:
                    dve.wait_ge(vchain, chained[0])
                link(v.bn_aggr(lag[:, c, :], lst[:, c, :]))
                v.tensor_scalar(lnm[:, 0, c:c + 1], lag[:, c, 0:1], -1.0, None, ALU.mult)
                variance(c)
                if c == 1:
                    w_part(7)
            dve.wait_ge(free_act, releaser[:uses[("bb", NBB - 1)] + 1].count("act"))
            v.memset(hlT[:, :, :, N:N2].bitcast(F32), 0.0)

            def x1_lo(c):
                dve.wait_ge(t_hi, c + 1)
                n = slice(c * PC, (c + 1) * PC)
                ins = v.tensor_tensor(hlT[:, 1, :, n], bank(("x1T", c))[:, 0:KC * PC].rearrange("p (k n) -> p k n", k=KC),
                                      hlT[:, 0, :, n].bitcast(F32), ALU.subtract)
                link(ins)
                dve.sem_inc(free_dve, 1)
                dve.sem_inc(t_ready, 1)

            for c in range(EARLY):
                x1_lo(c)
            w_part(8)
            for c in range(EARLY, NC):
                x1_lo(c)
            gw = vecT[:, 0, :, V_GATE:V_GATE + 2 * R].rearrange("p k (l r) -> p l k r", l=2)
            link(v.tensor_copy(gw_hl[:, :, :, 0], gw))
            v.tensor_tensor(gw_hl[:, :, :, 1], gw, gw_hl[:, :, :, 0].bitcast(F32), ALU.subtract).then_inc(gw_ready, 1)
            w_part(9)
            w_part(10)

            def z_parts(L):
                dve.wait_ge(gate_ready, L + 1)
                for c in range(NC):
                    for r in range(R):
                        u = (L * NC + c) * R + r
                        dve.wait_ge(zg_hi, u + 1)
                        link(v.scalar_tensor_tensor(out=zg[:, 1, c, r, :], in0=bank(("Z", L, c, r))[0:PC, :],
                                                    scalar=gate[:, L, c, r:r + 1], in1=zg[:, 0, c, r, :].bitcast(F32),
                                                    op0=ALU.mult, op1=ALU.subtract))
                        dve.sem_inc(free_dve, 1)
                        dve.sem_inc(zg_ready, 1)
                    if L == 0 and c in (0, 2, 4):
                        w_part(11 + c // 2)
                    if L == 1 and c == 2:
                        dve.wait_ge(root_hi, KC + 1)
                        v.tensor_tensor(root2_lo[:], root2_raw[:], root2_hi[:].bitcast(F32), ALU.subtract) \
                            .then_inc(root_ready, 1)

            z_parts(0)
            for h, (a, n) in enumerate(HALF):
                n = min(n, N - a)
                for f in range(KC):
                    i = KC * h + f
                    wait_full(dve, ("h", f, h))
                    t = r1T[:, f, a:a + n]
                    link(v.tensor_tensor(t, t, bank(("h", f, h))[:, 0:n], ALU.add))
                    dve.sem_inc(free_dve, 1)
                    dve.sem_inc(h_sum, 1)
                    dve.wait_ge(t_hi, NC + i + 1)
                    v.scalar_tensor_tensor(out=hlT[:, 1, f, a:a + n], in0=t, scalar=0.0,
                                           in1=hlT[:, 0, f, a:a + n].bitcast(F32), op0=ALU.max, op1=ALU.subtract) \
                        .then_inc(t_ready, 1)
                    if i in (2, 4):
                        w_part(13 + i // 2)
            z_parts(1)
            dve.wait_ge(bias2_in, 16)
            dve.wait_ge(basis_used, 2 * CH * SUB)
            for c in range(NC):
                t = res[:, c, :].rearrange("p (k c u) -> p k c u", k=KB, c=KC)
                link(v.tensor_tensor(t, q_as_natural(xs[:, c, :]),
                                     bias2_b[:].rearrange("p (k c u) -> p k c u", k=KB, c=KC), ALU.add))
                wait_full(dve, ("out", c))
                link(v.tensor_tensor(res[:, c, :], res[:, c, :], bank(("out", c))[0:PC, :], ALU.add))
                dve.sem_inc(free_dve, 1)
                statistics(c, res[:, c, :])
                variance(c)
                if c:
                    normalise(c - 1, res[:, c - 1, :], o_ready)
            normalise(NC - 1, res[:, NC - 1, :], o_ready)


_INS = ["x", "src", "dst", "edge_type_2", "L0_gnn_W", "L0_gnn_b", "L0_gnn_gamma", "L0_gnn_beta",
        "L1_gnn_basis1", "L1_gnn_att1", "L1_gnn_gate_w1", "L1_gnn_root1", "L1_gnn_bias1",
        "L1_gnn_basis2", "L1_gnn_att2", "L1_gnn_gate_w2", "L1_gnn_root2", "L1_gnn_bias2"]


def kernel(**inputs):
    import concourse.bacc as _bacc
    from concourse.bass_utils import run_bass_kernel_spmd as _run

    nc = _bacc.Bacc("TRN2", target_bir_lowering=False, num_devices=1)
    arrays, args = {}, []
    for name in _INS:
        a = np.ascontiguousarray(inputs[name])
        arrays[f"in_{name}_dram"] = a
        args.append(nc.dram_tensor(f"in_{name}_dram", a.shape, mybir.dt.from_np(a.dtype), kind="ExternalInput").ap())
    out = nc.dram_tensor("out_0_dram", (N, D), F32, kind="ExternalOutput").ap()
    gnn_block(nc, *args, out)
    r = _run(nc, [arrays], core_ids=[0])
    return r.results[0]["out_0_dram"]
```
